# Optimizing a Trainium2 kernel written in Bass

```python
import numpy as np
import jax
import jax.numpy as jnp

def _softmax(x, axis=-1):
    return jax.nn.softmax(x, axis=axis)

def _gelu(x):
    return jax.nn.gelu(x, approximate=True)

def _silu(x):
    return jax.nn.silu(x)

def _sigmoid(x):
    return jax.nn.sigmoid(x)

def _layernorm(x, axis=-1, eps=1e-05):
    m = jnp.mean(x, axis=axis, keepdims=True)
    v = jnp.var(x, axis=axis, keepdims=True)
    return (x - m) / jnp.sqrt(v + eps)

def _scatter_add(tgt, idx, src, axis=0):
    return tgt.at[idx].add(src)

def _segment_sum(src, seg, n):
    return jax.ops.segment_sum(src, seg, n)
kernel_name = 'mk_prb_d2_jaxref_r8_b79b87'

def setup_inputs(seed: int=0):
    np.random.seed(seed)
    _w = jnp.asarray

    def _L0_attn_setup():
        import jax, jax.numpy as jnp
        import numpy as np
        B, T, D = (2, 256, 256)
        H = 8
        KEY_DIM, VAL_DIM = (128, 256)
        HK, HV = (KEY_DIM // H, VAL_DIM // H)
        LOW_RANK = 16
        GATE_NORM = 16.0
        CHUNK = 64
        HIDDEN = (D * 4 * 2 // 3 + 63) // 64 * 64
        EPS = 1e-06

        def rmsnorm(x, w):
            return x * jax.lax.rsqrt(jnp.mean(x * x, axis=-1, keepdims=True) + EPS) * w

        def _gla(h, wq, wk, wv, gk_w1, gk_w2, gk_b, wg, gnorm_w, wo):
            Bb, Tt, _ = h.shape
            nc = Tt // CHUNK

            def split(t, hd):
                t = t.reshape(Bb, nc, CHUNK, H, hd)
                return jnp.transpose(t, (1, 0, 3, 2, 4))
            q = split(h @ wq, HK) * HK ** (-0.5)
            k = split(h @ wk, HK)
            v = split(h @ wv, HV)
            g = split(jax.nn.log_sigmoid(h @ gk_w1 @ gk_w2 + gk_b) / GATE_NORM, HK)
            mask = jnp.tril(jnp.ones((CHUNK, CHUNK), jnp.float32))

            def step(S, inp):
                qc, kc, vc, gc = inp
                b = jnp.cumsum(gc, axis=-2)
                qe = qc * jnp.exp(b)
                A = jnp.einsum('bhik,bhjk->bhij', qe, kc * jnp.exp(-b)) * mask
                o = jnp.einsum('bhck,bhkv->bhcv', qe, S) + jnp.einsum('bhij,bhjv->bhiv', A, vc)
                bl = b[:, :, -1:, :]
                S = jnp.exp(bl[:, :, 0, :])[..., None] * S + jnp.einsum('bhck,bhcv->bhkv', kc * jnp.exp(bl - b), vc)
                return (S, o)
            S0 = jnp.zeros((Bb, H, HK, HV), h.dtype)
            _, o = jax.lax.scan(step, S0, (q, k, v, g))
            o = jnp.transpose(o, (1, 0, 3, 2, 4)).reshape(Bb, Tt, H, HV)
            gate = (h @ wg).reshape(Bb, Tt, H, HV)
            o = rmsnorm(o, gnorm_w) * gate * jax.nn.sigmoid(gate)
            return o.reshape(Bb, Tt, VAL_DIM) @ wo
        key = jax.random.key(seed)
        ks = jax.random.split(key, 12)
        w = lambda k, s: jax.random.normal(k, s, jnp.float32) * 0.02
        return {'x': jax.random.normal(ks[0], (B, T, D), jnp.float32), 'norm1_w': jnp.ones((D,), jnp.float32), 'wq': w(ks[1], (D, KEY_DIM)), 'wk': w(ks[2], (D, KEY_DIM)), 'wv': w(ks[3], (D, VAL_DIM)), 'gk_w1': w(ks[4], (D, LOW_RANK)), 'gk_w2': w(ks[5], (LOW_RANK, KEY_DIM)), 'gk_b': jnp.zeros((KEY_DIM,), jnp.float32), 'wg': w(ks[6], (D, VAL_DIM)), 'gnorm_w': jnp.ones((HV,), jnp.float32), 'wo': w(ks[7], (VAL_DIM, D)), 'ffn_norm_w': jnp.ones((D,), jnp.float32), 'w_gate': w(ks[8], (D, HIDDEN)), 'w_up': w(ks[9], (D, HIDDEN)), 'w_down': w(ks[10], (HIDDEN, D))}
    _L0_attn_in = _L0_attn_setup()

    def _L0_ffn_setup():
        import jax, jax.numpy as jnp
        import numpy as np
        TOPK = 2
        HID, INTER, E, SHARED_INTER = (256, 176, 14, 352)
        key = jax.random.key(seed)
        ks = jax.random.split(key, 11)
        s = 0.02
        return {'x': jax.random.normal(ks[0], (4, 64, HID), jnp.float32), 'gate_w': jax.random.normal(ks[1], (E, HID), jnp.float32) * s, 'cls_w': jax.random.normal(ks[2], (E, HID), jnp.float32) * s, 'extra_scale': jax.random.normal(ks[3], (E,), jnp.float32) * 0.1, 'extra_bias': jax.random.normal(ks[4], (E,), jnp.float32) * 0.01, 'wg': jax.random.normal(ks[5], (E, INTER, HID), jnp.float32) * s, 'wu': jax.random.normal(ks[6], (E, INTER, HID), jnp.float32) * s, 'wd': jax.random.normal(ks[7], (E, HID, INTER), jnp.float32) * s, 'sg': jax.random.normal(ks[8], (SHARED_INTER, HID), jnp.float32) * s, 'su': jax.random.normal(ks[9], (SHARED_INTER, HID), jnp.float32) * s, 'sd': jax.random.normal(ks[10], (HID, SHARED_INTER), jnp.float32) * s}
    _L0_ffn_in = _L0_ffn_setup()

    def _L1_attn_setup():
        import jax, jax.numpy as jnp
        import numpy as np
        DIM = 256
        D_STATE = 128
        D_CONV = 4
        N_HEADS = 48
        N_GROUPS = 1
        D_HEAD = 64
        D_INNER = N_HEADS * D_HEAD
        EPS = 1e-05
        RES_MULT = 1.0
        SEQ = 128
        BATCH = 1

        def _rms(x, w, eps=EPS):
            return x * jax.lax.rsqrt(jnp.mean(x * x, axis=-1, keepdims=True) + eps) * w

        def _forward(x, norm_w, in_proj_w, conv_w, conv_b, dt_bias, A_log, D_param, inner_norm_w, out_proj_w, conv_state, ssm_state):
            b, s, _ = x.shape
            xn = _rms(x, norm_w)
            proj = xn @ in_proj_w.T
            gn = N_GROUPS * D_STATE
            z, xc, B, C, dt = jnp.split(proj, [D_INNER, 2 * D_INNER, 2 * D_INNER + gn, 2 * D_INNER + 2 * gn], axis=-1)
            xc = jnp.moveaxis(xc, 1, 2)
            xp = jnp.concatenate([jnp.broadcast_to(conv_state, (b, D_INNER, D_CONV - 1)), xc], axis=-1)
            conv_out = conv_b[None, :, None] + sum((conv_w[None, :, k, None] * xp[:, :, k:k + s] for k in range(D_CONV)))
            xc = jax.nn.silu(conv_out)
            x_ssm = jnp.moveaxis(xc, 1, 2).reshape(b, s, N_HEADS, D_HEAD)
            hpg = N_HEADS // N_GROUPS
            B = jnp.repeat(B.reshape(b, s, N_GROUPS, D_STATE), hpg, axis=2)
            C = jnp.repeat(C.reshape(b, s, N_GROUPS, D_STATE), hpg, axis=2)
            dt = jax.nn.softplus(dt + dt_bias)
            A = -jnp.exp(A_log)
            h0 = jnp.broadcast_to(ssm_state, (b, N_HEADS, D_STATE, D_HEAD))

            def step(h, ins):
                x_t, B_t, C_t, dt_t = ins
                dA = jnp.exp(A * dt_t)[..., None, None]
                h = dA * h + B_t[..., :, None] * x_t[..., None, :]
                y_t = jnp.einsum('bhnp,bhn->bhp', h, C_t) + D_param[None, :, None] * x_t
                return (h, y_t)
            _, ys = jax.lax.scan(step, h0, (jnp.moveaxis(x_ssm, 1, 0), jnp.moveaxis(B, 1, 0), jnp.moveaxis(C, 1, 0), jnp.moveaxis(dt, 1, 0)))
            y = jnp.moveaxis(ys, 0, 1).reshape(b, s, D_INNER)
            y = _rms(y, inner_norm_w)
            y = y * jax.nn.silu(z)
            out = y @ out_proj_w.T
            return x + out * RES_MULT
        key = jax.random.key(seed)
        ks = jax.random.split(key, 12)
        d_in_proj = 2 * D_INNER + 2 * N_GROUPS * D_STATE + N_HEADS
        return {'x': jax.random.normal(ks[0], (BATCH, SEQ, DIM), jnp.float32), 'norm_w': jnp.ones((DIM,), jnp.float32), 'in_proj_w': 0.02 * jax.random.normal(ks[1], (d_in_proj, DIM), jnp.float32), 'conv_w': 0.02 * jax.random.normal(ks[2], (D_INNER, D_CONV), jnp.float32), 'conv_b': 0.01 * jax.random.normal(ks[3], (D_INNER,), jnp.float32), 'dt_bias': 0.1 * jax.random.normal(ks[4], (N_HEADS,), jnp.float32), 'A_log': 0.1 * jax.random.normal(ks[5], (N_HEADS,), jnp.float32), 'D_param': 0.1 * jax.random.normal(ks[6], (N_HEADS,), jnp.float32), 'inner_norm_w': jnp.ones((D_INNER,), jnp.float32), 'out_proj_w': 0.02 * jax.random.normal(ks[7], (DIM, D_INNER), jnp.float32), 'conv_state': jnp.zeros((1, D_INNER, D_CONV - 1), jnp.float32), 'ssm_state': jnp.zeros((1, N_HEADS, D_STATE, D_HEAD), jnp.float32)}
    _L1_attn_in = _L1_attn_setup()

    def _L1_ffn_setup():
        import jax, jax.numpy as jnp
        import numpy as np
        B, T, D, F, E, K = (2, 128, 256, 96, 16, 2)
        key = jax.random.key(seed)
        k0, k1, k2, k3, k4 = jax.random.split(key, 5)
        scale = 0.02
        return {'x': jax.random.normal(k0, (B, T, D), dtype=jnp.float32), 'router_w': jax.random.normal(k1, (D, E), dtype=jnp.float32) * scale, 'gate_w': jax.random.normal(k2, (E, D, F), dtype=jnp.float32) * scale, 'up_w': jax.random.normal(k3, (E, D, F), dtype=jnp.float32) * scale, 'down_w': jax.random.normal(k4, (E, F, D), dtype=jnp.float32) * scale}
    _L1_ffn_in = _L1_ffn_setup()
    _d = {'L0_attn_x': _L0_attn_in['x'], 'L0_attn_norm1_w': _L0_attn_in['norm1_w'], 'L0_attn_wq': _L0_attn_in['wq'], 'L0_attn_wk': _L0_attn_in['wk'], 'L0_attn_wv': _L0_attn_in['wv'], 'L0_attn_gk_w1': _L0_attn_in['gk_w1'], 'L0_attn_gk_w2': _L0_attn_in['gk_w2'], 'L0_attn_gk_b': _L0_attn_in['gk_b'], 'L0_attn_wg': _L0_attn_in['wg'], 'L0_attn_gnorm_w': _L0_attn_in['gnorm_w'], 'L0_attn_wo': _L0_attn_in['wo'], 'L0_attn_ffn_norm_w': _L0_attn_in['ffn_norm_w'], 'L0_attn_w_gate': _L0_attn_in['w_gate'], 'L0_attn_w_up': _L0_attn_in['w_up'], 'L0_attn_w_down': _L0_attn_in['w_down'], 'L0_ffn_gate_w': _L0_ffn_in['gate_w'], 'L0_ffn_cls_w': _L0_ffn_in['cls_w'], 'L0_ffn_extra_scale': _L0_ffn_in['extra_scale'], 'L0_ffn_extra_bias': _L0_ffn_in['extra_bias'], 'L0_ffn_wg': _L0_ffn_in['wg'], 'L0_ffn_wu': _L0_ffn_in['wu'], 'L0_ffn_wd': _L0_ffn_in['wd'], 'L0_ffn_sg': _L0_ffn_in['sg'], 'L0_ffn_su': _L0_ffn_in['su'], 'L0_ffn_sd': _L0_ffn_in['sd'], 'L1_attn_norm_w': _L1_attn_in['norm_w'], 'L1_attn_in_proj_w': _L1_attn_in['in_proj_w'], 'L1_attn_conv_w': _L1_attn_in['conv_w'], 'L1_attn_conv_b': _L1_attn_in['conv_b'], 'L1_attn_dt_bias': _L1_attn_in['dt_bias'], 'L1_attn_A_log': _L1_attn_in['A_log'], 'L1_attn_D_param': _L1_attn_in['D_param'], 'L1_attn_inner_norm_w': _L1_attn_in['inner_norm_w'], 'L1_attn_out_proj_w': _L1_attn_in['out_proj_w'], 'L1_attn_conv_state': _L1_attn_in['conv_state'], 'L1_attn_ssm_state': _L1_attn_in['ssm_state'], 'L1_ffn_router_w': _L1_ffn_in['router_w'], 'L1_ffn_gate_w': _L1_ffn_in['gate_w'], 'L1_ffn_up_w': _L1_ffn_in['up_w'], 'L1_ffn_down_w': _L1_ffn_in['down_w']}
    _x0 = _d['L0_attn_x']
    _d['L0_attn_x'] = jax.random.normal(jax.random.fold_in(jax.random.key(seed), 1), (2, 2048, 256), dtype=_x0.dtype)
    del _x0
    return _d

def reference(L0_attn_x, L0_attn_norm1_w, L0_attn_wq, L0_attn_wk, L0_attn_wv, L0_attn_gk_w1, L0_attn_gk_w2, L0_attn_gk_b, L0_attn_wg, L0_attn_gnorm_w, L0_attn_wo, L0_attn_ffn_norm_w, L0_attn_w_gate, L0_attn_w_up, L0_attn_w_down, L0_ffn_gate_w, L0_ffn_cls_w, L0_ffn_extra_scale, L0_ffn_extra_bias, L0_ffn_wg, L0_ffn_wu, L0_ffn_wd, L0_ffn_sg, L0_ffn_su, L0_ffn_sd, L1_attn_norm_w, L1_attn_in_proj_w, L1_attn_conv_w, L1_attn_conv_b, L1_attn_dt_bias, L1_attn_A_log, L1_attn_D_param, L1_attn_inner_norm_w, L1_attn_out_proj_w, L1_attn_conv_state, L1_attn_ssm_state, L1_ffn_router_w, L1_ffn_gate_w, L1_ffn_up_w, L1_ffn_down_w):

    def _L0_attn_ref(x, norm1_w, wq, wk, wv, gk_w1, gk_w2, gk_b, wg, gnorm_w, wo, ffn_norm_w, w_gate, w_up, w_down):
        import jax, jax.numpy as jnp
        import numpy as np
        B, T, D = (2, 256, 256)
        H = 8
        KEY_DIM, VAL_DIM = (128, 256)
        HK, HV = (KEY_DIM // H, VAL_DIM // H)
        LOW_RANK = 16
        GATE_NORM = 16.0
        CHUNK = 64
        HIDDEN = (D * 4 * 2 // 3 + 63) // 64 * 64
        EPS = 1e-06

        def rmsnorm(x, w):
            return x * jax.lax.rsqrt(jnp.mean(x * x, axis=-1, keepdims=True) + EPS) * w

        def _gla(h, wq, wk, wv, gk_w1, gk_w2, gk_b, wg, gnorm_w, wo):
            Bb, Tt, _ = h.shape
            nc = Tt // CHUNK

            def split(t, hd):
                t = t.reshape(Bb, nc, CHUNK, H, hd)
                return jnp.transpose(t, (1, 0, 3, 2, 4))
            q = split(h @ wq, HK) * HK ** (-0.5)
            k = split(h @ wk, HK)
            v = split(h @ wv, HV)
            g = split(jax.nn.log_sigmoid(h @ gk_w1 @ gk_w2 + gk_b) / GATE_NORM, HK)
            mask = jnp.tril(jnp.ones((CHUNK, CHUNK), jnp.float32))

            def step(S, inp):
                qc, kc, vc, gc = inp
                b = jnp.cumsum(gc, axis=-2)
                qe = qc * jnp.exp(b)
                A = jnp.einsum('bhik,bhjk->bhij', qe, kc * jnp.exp(-b)) * mask
                o = jnp.einsum('bhck,bhkv->bhcv', qe, S) + jnp.einsum('bhij,bhjv->bhiv', A, vc)
                bl = b[:, :, -1:, :]
                S = jnp.exp(bl[:, :, 0, :])[..., None] * S + jnp.einsum('bhck,bhcv->bhkv', kc * jnp.exp(bl - b), vc)
                return (S, o)
            S0 = jnp.zeros((Bb, H, HK, HV), h.dtype)
            _, o = jax.lax.scan(step, S0, (q, k, v, g))
            o = jnp.transpose(o, (1, 0, 3, 2, 4)).reshape(Bb, Tt, H, HV)
            gate = (h @ wg).reshape(Bb, Tt, H, HV)
            o = rmsnorm(o, gnorm_w) * gate * jax.nn.sigmoid(gate)
            return o.reshape(Bb, Tt, VAL_DIM) @ wo
        h = rmsnorm(x, norm1_w)
        x = x + _gla(h, wq, wk, wv, gk_w1, gk_w2, gk_b, wg, gnorm_w, wo)
        h2 = rmsnorm(x, ffn_norm_w)
        ffn = jax.nn.silu(h2 @ w_gate) * (h2 @ w_up) @ w_down
        return x + ffn

    def _L0_ffn_ref(x, gate_w, cls_w, extra_scale, extra_bias, wg, wu, wd, sg, su, sd):
        import jax, jax.numpy as jnp
        import numpy as np
        TOPK = 2
        HID, INTER, E, SHARED_INTER = (256, 176, 14, 352)
        shape = x.shape
        d = shape[-1]
        xf = x.reshape(-1, d)
        T = xf.shape[0]
        n_exp = gate_w.shape[0]
        logits = xf @ cls_w.T * jax.nn.silu(xf @ gate_w.T)
        scores = jax.nn.softmax(jnp.abs(logits).astype(jnp.float32), axis=-1)
        biased = scores + extra_bias[None, :]
        _, idx = jax.lax.top_k(biased, TOPK)
        orig = 1.0 + scores * extra_scale[None, :]
        w = jnp.take_along_axis(orig, idx, axis=1).astype(x.dtype)
        combine = jnp.zeros((T, n_exp), x.dtype).at[jnp.arange(T)[:, None], idx].add(w)
        g = jax.nn.silu(jnp.einsum('td,efd->etf', xf, wg))
        u = jnp.einsum('td,efd->etf', xf, wu)
        o = jnp.einsum('etf,edf->etd', g * u, wd)
        y = jnp.einsum('etd,te->td', o, combine)
        z = jax.nn.silu(xf @ sg.T) * (xf @ su.T) @ sd.T
        return (y + z).reshape(shape)

    def _L1_attn_ref(x, norm_w, in_proj_w, conv_w, conv_b, dt_bias, A_log, D_param, inner_norm_w, out_proj_w, conv_state, ssm_state):
        import jax, jax.numpy as jnp
        import numpy as np
        DIM = 256
        D_STATE = 128
        D_CONV = 4
        N_HEADS = 48
        N_GROUPS = 1
        D_HEAD = 64
        D_INNER = N_HEADS * D_HEAD
        EPS = 1e-05
        RES_MULT = 1.0
        SEQ = 128
        BATCH = 1

        def _rms(x, w, eps=EPS):
            return x * jax.lax.rsqrt(jnp.mean(x * x, axis=-1, keepdims=True) + eps) * w

        def _forward(x, norm_w, in_proj_w, conv_w, conv_b, dt_bias, A_log, D_param, inner_norm_w, out_proj_w, conv_state, ssm_state):
            b, s, _ = x.shape
            xn = _rms(x, norm_w)
            proj = xn @ in_proj_w.T
            gn = N_GROUPS * D_STATE
            z, xc, B, C, dt = jnp.split(proj, [D_INNER, 2 * D_INNER, 2 * D_INNER + gn, 2 * D_INNER + 2 * gn], axis=-1)
            xc = jnp.moveaxis(xc, 1, 2)
            xp = jnp.concatenate([jnp.broadcast_to(conv_state, (b, D_INNER, D_CONV - 1)), xc], axis=-1)
            conv_out = conv_b[None, :, None] + sum((conv_w[None, :, k, None] * xp[:, :, k:k + s] for k in range(D_CONV)))
            xc = jax.nn.silu(conv_out)
            x_ssm = jnp.moveaxis(xc, 1, 2).reshape(b, s, N_HEADS, D_HEAD)
            hpg = N_HEADS // N_GROUPS
            B = jnp.repeat(B.reshape(b, s, N_GROUPS, D_STATE), hpg, axis=2)
            C = jnp.repeat(C.reshape(b, s, N_GROUPS, D_STATE), hpg, axis=2)
            dt = jax.nn.softplus(dt + dt_bias)
            A = -jnp.exp(A_log)
            h0 = jnp.broadcast_to(ssm_state, (b, N_HEADS, D_STATE, D_HEAD))

            def step(h, ins):
                x_t, B_t, C_t, dt_t = ins
                dA = jnp.exp(A * dt_t)[..., None, None]
                h = dA * h + B_t[..., :, None] * x_t[..., None, :]
                y_t = jnp.einsum('bhnp,bhn->bhp', h, C_t) + D_param[None, :, None] * x_t
                return (h, y_t)
            _, ys = jax.lax.scan(step, h0, (jnp.moveaxis(x_ssm, 1, 0), jnp.moveaxis(B, 1, 0), jnp.moveaxis(C, 1, 0), jnp.moveaxis(dt, 1, 0)))
            y = jnp.moveaxis(ys, 0, 1).reshape(b, s, D_INNER)
            y = _rms(y, inner_norm_w)
            y = y * jax.nn.silu(z)
            out = y @ out_proj_w.T
            return x + out * RES_MULT
        return _forward(x, norm_w, in_proj_w, conv_w, conv_b, dt_bias, A_log, D_param, inner_norm_w, out_proj_w, conv_state, ssm_state)

    def _L1_ffn_ref(x, router_w, gate_w, up_w, down_w):
        import jax, jax.numpy as jnp
        import numpy as np
        B, T, D, F, E, K = (2, 128, 256, 96, 16, 2)
        scores = jnp.einsum('btd,de->bte', x, router_w).astype(jnp.float32)
        probs = jax.nn.softmax(scores, axis=-1)
        routing_weights, routing_idx = jax.lax.top_k(probs, K)
        routing_weights = routing_weights / jnp.sum(routing_weights, axis=-1, keepdims=True)
        routing_weights = routing_weights.astype(x.dtype)
        one_hot = jax.nn.one_hot(routing_idx, E, dtype=x.dtype)
        combine = jnp.einsum('btk,btke->bte', routing_weights, one_hot)
        g = jnp.einsum('btd,edf->ebtf', x, gate_w)
        u = jnp.einsum('btd,edf->ebtf', x, up_w)
        h = jax.nn.silu(g) * u
        expert_out = jnp.einsum('ebtf,efd->ebtd', h, down_w)
        out = jnp.einsum('ebtd,bte->btd', expert_out, combine)
        return out
    x = L0_attn_x
    xn = _layernorm(x, axis=-1)
    x = x + _L0_attn_ref(xn, L0_attn_norm1_w, L0_attn_wq, L0_attn_wk, L0_attn_wv, L0_attn_gk_w1, L0_attn_gk_w2, L0_attn_gk_b, L0_attn_wg, L0_attn_gnorm_w, L0_attn_wo, L0_attn_ffn_norm_w, L0_attn_w_gate, L0_attn_w_up, L0_attn_w_down) + _L0_ffn_ref(xn, L0_ffn_gate_w, L0_ffn_cls_w, L0_ffn_extra_scale, L0_ffn_extra_bias, L0_ffn_wg, L0_ffn_wu, L0_ffn_wd, L0_ffn_sg, L0_ffn_su, L0_ffn_sd)
    xn = _layernorm(x, axis=-1)
    x = x + _L1_attn_ref(xn, L1_attn_norm_w, L1_attn_in_proj_w, L1_attn_conv_w, L1_attn_conv_b, L1_attn_dt_bias, L1_attn_A_log, L1_attn_D_param, L1_attn_inner_norm_w, L1_attn_out_proj_w, L1_attn_conv_state, L1_attn_ssm_state) + _L1_ffn_ref(xn, L1_ffn_router_w, L1_ffn_gate_w, L1_ffn_up_w, L1_ffn_down_w)
    return x

_drawn_inputs = setup_inputs


def setup_inputs(seed=0):
    import zlib

    import numpy as np

    out = dict(_drawn_inputs(seed))
    spreads = {'L0_attn_norm1_w': (1.0, 0.6),
     'L0_attn_gk_b': (0.0, 0.8),
     'L0_attn_gnorm_w': (1.0, 0.6),
     'L0_attn_ffn_norm_w': (1.0, 0.6),
     'L1_attn_norm_w': (1.0, 0.6),
     'L1_attn_inner_norm_w': (1.0, 0.6),
     'L1_attn_conv_state': (0.0, 2.0),
     'L1_attn_ssm_state': (0.0, 2.0)}
    factors = {'L0_attn_gk_w1': 8.0,
     'L0_attn_gk_w2': 8.0,
     'L0_attn_w_gate': 3.667,
     'L0_attn_w_up': 3.631,
     'L0_attn_w_down': 3.631,
     'L0_ffn_gate_w': 8.0,
     'L0_ffn_cls_w': 8.0,
     'L0_ffn_extra_scale': 8.0,
     'L0_ffn_extra_bias': 6.478,
     'L0_ffn_wg': 5.725,
     'L0_ffn_wu': 5.65,
     'L0_ffn_wd': 5.642,
     'L0_ffn_sg': 5.747,
     'L0_ffn_su': 5.692,
     'L0_ffn_sd': 5.68,
     'L1_attn_dt_bias': 30.292,
     'L1_attn_A_log': 23.798,
     'L1_attn_D_param': 200.0,
     'L1_ffn_router_w': 8.0,
     'L1_ffn_gate_w': 8.0,
     'L1_ffn_up_w': 8.0,
     'L1_ffn_down_w': 8.0,
     'L1_attn_conv_b': 14.797,
     'L1_attn_conv_w': 6.642}
    for name, (base, spread) in spreads.items():
        noise = np.random.default_rng([zlib.crc32(name.encode()), seed]).standard_normal(out[name].shape)
        drawn = base * np.exp(spread * noise) if base else spread * noise
        out[name] = jnp.asarray(drawn.astype(out[name].dtype))
    for name, factor in factors.items():
        out[name] = (out[name] * factor).astype(out[name].dtype)
    return out
```

```python
from contextlib import ExitStack

import concourse.bass as bass
from concourse import mybir

F32 = mybir.dt.float32
F32R = mybir.dt.float32r
U32 = mybir.dt.uint32
ACT = mybir.ActivationFunctionType
ALU = mybir.AluOpType
AX = mybir.AxisListType

P = 128
B, T, D = 2, 2048, 256
KD = D // P
TS = 512
NS = T // TS
NJ = TS // P

H0, HK, HV, CH = 8, 16, 32, 64
NC0 = TS // CH
LR = 16
GNORM = 16.0
E0, NE = 14, 16
HM, PH, NST = 48, 64, 128
DI = HM * PH
NCT = DI // P
NR = 4
MLP_W = 2 * KD * P + D
MP_IN, MP_OUT = 2 * KD * P, D
MP_VEC = MP_IN + MP_OUT
MP_CS = MP_VEC + 8
MP_ST = MP_CS + 4
MP_W = MP_ST + P

_cols = {}
_at = 0
for _n, _w in (("ident", P), ("mean", P), ("mean32", P), ("mean_di", P), ("scan64", TS), ("scan128", TS),
               ("causal64", CH), ("causal128", P), ("headmask", H0), ("bdmask", D), ("iota", NE),
               ("bias0", E0), ("scale0", E0), ("norm1", KD), ("ffn_norm", KD), ("norm_m", KD),
               ("gk_b", 1), ("gnorm", 1), ("dt_bias", 1), ("A_log", 1),
               ("router0", KD * 2 * E0), ("router1", KD * NE), ("gk1", KD * LR), ("gk2", P), ("wdt", KD * HM)):
    _cols[_n] = (_at, _at + _w)
    _at += _w
TABLE_W = _at


def mm3(pe, out, w, x, first=True, last=True):
    (wh, wl), (xh, xl) = w, x
    pe.matmul(out, wh, xh, start=first, stop=False)
    pe.matmul(out, wh, xl, start=False, stop=False)
    return pe.matmul(out, wl, xh, start=False, stop=last)


class Phase:

    def __init__(self, nc, pool):
        self.nc, self.pool, self.names = nc, pool, {}

    def __getitem__(self, name):
        if name not in self.names:
            self.names[name] = self.pool[len(self.names)]
        return self.names[name]

    def clear(self):
        first = self.pool[0].num
        self.nc.sync.sem_clear(range(first, first + len(self.names)))
        self.nc.all_engine_barrier(sem_only=True)


def need(eng, sig, **counts):
    for name, n in counts.items():
        eng.wait_ge(sig[name], n)


def program(nc, xT, table, gla_w, gla_wo, wbc, moe0, ffn0, moe1, mamba, a_dram, outT):
    ctx = ExitStack()
    with ctx:
        pool = [ctx.enter_context(nc.semaphore(f"sig{i}")) for i in range(100)]
        assert [s.num for s in pool] == list(range(pool[0].num, pool[0].num + len(pool)))

        def sb(name, shape, dt=F32, where=ctx):
            return where.enter_context(nc.sbuf_tensor(name, shape, dt))

        bank = ctx.enter_context(nc.psum_tensor("bank", [P, 8, TS], F32))

        tab = sb("tab", [P, TABLE_W])
        acc = sb("acc", [P, KD, T])
        f_hi = sb("f_hi", [P, KD, T], F32R)
        f_lo = sb("f_lo", [P, KD, T], F32R)

        def col(name):
            a, b = _cols[name]
            return tab[:, a:b]

        def colk(name, k=KD):
            return col(name).rearrange("p (k c) -> p k c", k=k)

        ident = col("ident")

        with nc.Block(no_gpsimd_drain=True) as block:
            ph = Phase(nc, pool)

            @block.sync
            def _(sp):
                sp.dma_start(tab[:], table).then_inc(ph["table"], 16)
                sp.wait_ge(ph["table"], 16)
        ph.clear()

        with nc.Fori(0, B) as b:
            with ExitStack() as own:
                e_hi = sb("e_hi", [P, KD, T], F32R, own)
                e_lo = sb("e_lo", [P, KD, T], F32R, own)
                cw = sb("cw", [P, T], F32, own)
                attention(nc, pool, bank, b, xT, gla_w, gla_wo, acc, e_hi, e_lo, f_hi, f_lo, cw, col, colk)
                mlp(nc, pool, bank, "ffn", ffn0, f_hi, f_lo, None, acc)
                mlp(nc, pool, bank, "moe0", moe0, e_hi, e_lo, cw, acc)
            with ExitStack() as layer1:
                st = {n: sb(n, shape, F32, layer1) for n, shape in (
                    ("b_tok", [P, T // P, NST]),
                    ("c_feat", [P, T]),
                    ("cb", [P, T // P, P]),
                    ("a_tok", [P, T // P, HM]),
                    ("w_tok", [P, T // P, HM]))}
                with ExitStack() as own:
                    e_hi = sb("e1_hi", [P, KD, T], F32R, own)
                    e_lo = sb("e1_lo", [P, KD, T], F32R, own)
                    cw = sb("cw1", [P, T], F32, own)
                    ssm_prepare(nc, pool, bank, wbc, a_dram, acc, e_hi, e_lo, f_hi, f_lo, cw, st, col, colk)
                    mlp(nc, pool, bank, "moe1", moe1, e_hi, e_lo, cw, acc)
                ssm(nc, pool, bank, mamba, a_dram, acc, f_hi, f_lo, st, col)
            with nc.Block(no_gpsimd_drain=True) as block:
                ph = Phase(nc, pool)

                @block.sync
                def _(sp):
                    sp.dma_start(outT[bass.ds(b, 1)].rearrange("o p k t -> (o p) k t"), acc[:]).then_inc(ph["out"], 16)
                    sp.wait_ge(ph["out"], 16)
            ph.clear()


def attention(nc, pool, bank, b, xT, gla_w, gla_wo, acc, e_hi, e_lo, f_hi, f_lo, cw, col, colk):
    with ExitStack() as own:
        def sb(name, shape, dt=F32):
            return own.enter_context(nc.sbuf_tensor(name, shape, dt))

        w_hi, w_lo = sb("gw_hi", [P, KD, 768], F32R), sb("gw_lo", [P, KD, 768], F32R)
        wo_hi, wo_lo = sb("gwo_hi", [P, KD, D], F32R), sb("gwo_lo", [P, KD, D], F32R)
        state = sb("state", [P, 2, D])
        ph = Phase(nc, pool)
        with (nc.sbuf_tensor("gw_raw", [P, KD, 768], F32) as w_raw, nc.sbuf_tensor("gwo_raw", [P, KD, D], F32) as wo_raw,
              nc.Block(no_gpsimd_drain=True) as block):
            @block.sync
            def _(sp):
                sp.dma_start(w_raw[:], gla_w).then_inc(ph["raw"], 16)
                sp.dma_start(wo_raw[:], gla_wo).then_inc(ph["raw"], 16)
                sp.wait_ge(ph["raw"], 32)

            @block.vector
            def _(dve):
                dve.memset(state[:], 0.0)
                dve.wait_ge(ph["raw"], 32)
                dve.tensor_copy(w_hi[:], w_raw[:]).then_inc(ph["hi"], 1)
                dve.tensor_copy(wo_hi[:], wo_raw[:]).then_inc(ph["hi"], 1)
                dve.wait_ge(ph["hi"], 2)
                dve.tensor_tensor(w_lo[:], w_raw[:], w_hi[:].bitcast(F32), ALU.subtract)
                dve.tensor_tensor(wo_lo[:], wo_raw[:], wo_hi[:].bitcast(F32), ALU.subtract)
        ph.clear()

        x = sb("x", [P, KD, TS])
        xc = sb("xc", [P, KD, TS])
        sq = sb("sq", [P, KD, TS])
        r = sb("r", [P, 6, TS])
        xn = sb("xn", [P, KD, TS])
        h = sb("h", [P, KD, TS])
        h_hi, h_lo = sb("h_hi", [P, KD, TS], F32R), sb("h_lo", [P, KD, TS], F32R)
        rt = router_tiles(sb, "rt0_")
        lowrank = sb("lowrank", [LR, TS])
        v = sb("v", [P, NJ, D])
        sgate = sb("sgate", [P, KD, TS])
        g = sb("g", [P, 8, TS])
        qe, ke, kl = sb("qe", [P, TS]), sb("ke", [P, TS]), sb("kl", [P, TS])
        klt = sb("klt", [P, NJ, P])
        qb = sb("qb", [P, 2, H0, CH])
        am = sb("am", [P, 2, H0, CH])
        um = sb("um", [P, 2, D])
        on = sb("on", [P, KD, TS])
        og_hi, og_lo = h_hi, h_lo

        def both(a):
            return a.unsqueeze(1).broadcast_to([P, KD, TS])

        def by_chunk(a):
            return a.rearrange("p (j u c) -> p j u c", j=NJ, u=2)

        def heads_out(gr):
            return bank[:, 0:2, gr * NJ * CH:(gr + 1) * NJ * CH].rearrange("p u (j c) -> p j u c", j=NJ)

        with nc.Fori(0, NS) as s:
            ph = Phase(nc, pool)
            t0 = s * TS
            ts = bass.ds(t0, TS)
            gk, mn, e1, l1, gs, cum, eb, enb = (g[:, i, :] for i in range(8))
            with nc.Block(no_gpsimd_drain=True) as block:

                @block.sync
                def _(sp):
                    sp.dma_start(x[:], xT[bass.ds(b, 1), :, :, ts].rearrange("o p k t -> (o p) k t"))\
                        .then_inc(ph["x"], 16)
                    sp.wait_ge(ph["x"], 16)

                @block.tensor
                def _(pe):
                    need(pe, ph, x=16)
                    for k in range(KD):
                        i = pe.matmul(bank[:, 0, :], col("mean"), x[:, k, :], start=k == 0, stop=k == KD - 1)
                    i.then_inc(ph["mean"], 1)
                    need(pe, ph, sq=1)
                    for k in range(KD):
                        i = pe.matmul(bank[:, 1, :], col("mean"), sq[:, k, :], start=k == 0, stop=k == KD - 1)
                    i.then_inc(ph["var"], 1)
                    need(pe, ph, xn=1)
                    router_logits(pe, ph, bank, xn, colk("router0"), 2 * E0)
                    need(pe, ph, h_hi=1, h_lo=1)
                    for n, dst in ((0, 4), (1, 5)):
                        for k in range(KD):
                            c = slice(n * P, n * P + P)
                            i = mm3(pe, bank[:, dst, :], (w_hi[:, k, c], w_lo[:, k, c]),
                                    (h_hi[:, k, :], h_lo[:, k, :]), k == 0, k == KD - 1)
                    i.then_inc(ph["qk"], 1)
                    for k in range(KD):
                        i = pe.matmul(bank[0:LR, 6, :], colk("gk1")[:, k, :], h[:, k, :], start=k == 0, stop=k == KD - 1)
                    i.then_inc(ph["rank_ps"], 1)
                    need(pe, ph, r1=1)
                    for j in range(NJ):
                        o = bank[:, j // 2, (j % 2) * D:(j % 2) * D + D]
                        for k in range(KD):
                            js = slice(j * P, j * P + P)
                            i = mm3(pe, o, (h_hi[:, k, js], h_lo[:, k, js]), (w_hi[:, k, 512:768], w_lo[:, k, 512:768]),
                                    k == 0, k == KD - 1)
                    i.then_inc(ph["v_ps"], 1)
                    need(pe, ph, rank=1)
                    pe.matmul(bank[:, 7, :], col("gk2")[0:LR, :], lowrank[:], start=True, stop=True).then_inc(ph["gk_ps"], 1)
                    router_transpose(pe, ph, bank, rt, col("ident"))
                    need(pe, ph, cw=1)
                    for n in range(KD):
                        for k in range(KD):
                            c = slice(256 + n * P, 256 + n * P + P)
                            i = mm3(pe, bank[:, 2 + n, :], (w_hi[:, k, c], w_lo[:, k, c]),
                                    (h_hi[:, k, :], h_lo[:, k, :]), k == 0, k == KD - 1)
                    i.then_inc(ph["gate_ps"], 1)
                    need(pe, ph, kl=1)
                    for j in range(NJ):
                        i = pe.transpose(bank[:, 6, j * P:(j + 1) * P], kl[:, j * P:(j + 1) * P], col("ident"))
                    i.then_inc(ph["klt_ps"], 1)
                    need(pe, ph, v=1, klt=1, ke=1)
                    for j in range(NJ):
                        a = bank[:, 4 + j % 2, :]
                        if j >= 2:
                            need(pe, ph, am=j - 1)
                        for u in range(2):
                            c = 2 * j + u
                            need(pe, ph, qb=c + 1)
                            i = pe.matmul(a[u * CH:(u + 1) * CH, :], ke[:, c * CH:(c + 1) * CH],
                                          qb[:, u].rearrange("p h c -> p (h c)"), start=True, stop=True)
                            i.then_inc(ph["a_ps"], 1)
                        for u in range(2):
                            c = 2 * j + u
                            rows = slice(u * CH, (u + 1) * CH)
                            if c >= 2:
                                need(pe, ph, um=c - 1)
                            pe.matmul(bank[:, 6 + u, 0:D], klt[rows, j, :], v[rows, j, :], start=True, stop=True)\
                                .then_inc(ph["u_ps"], 1)
                        need(pe, ph, am=j + 1)
                        for u in range(2):
                            c = 2 * j + u
                            rows = slice(u * CH, (u + 1) * CH)
                            if c:
                                need(pe, ph, state=c)
                            for gr in range(2):
                                o = bank[:, u, (gr * NJ + j) * CH:(gr * NJ + j + 1) * CH]
                                pe.matmul(o, state[:, c % 2, gr * P:(gr + 1) * P], qe[:, c * CH:(c + 1) * CH],
                                          start=True, stop=False)
                                for q in range(4):
                                    hh = 4 * gr + q
                                    i = pe.matmul(o[q * HV:(q + 1) * HV, :], v[rows, j, hh * HV:(hh + 1) * HV],
                                                  am[rows, j % 2, hh, :], start=False, stop=True,
                                                  tile_position=(u * CH, q * HV))
                            i.then_inc(ph["o_ps"], 1)
                    need(pe, ph, sqo=2)
                    for gr in range(2):
                        i = pe.matmul(bank[:, 4 + gr, :], col("mean32"), sq[:, gr, :], start=True, stop=True)
                    i.then_inc(ph["hms"], 1)
                    need(pe, ph, og_hi=1, og_lo=1)
                    for n in range(KD):
                        for k in range(KD):
                            c = slice(n * P, n * P + P)
                            i = mm3(pe, bank[:, 2 + n, :], (wo_hi[:, k, c], wo_lo[:, k, c]),
                                    (og_hi[:, k, :], og_lo[:, k, :]), k == 0, k == KD - 1)
                    i.then_inc(ph["gla_ps"], 1)
                    need(pe, ph, sqy=1)
                    for k in range(KD):
                        i = pe.matmul(bank[:, 6, :], col("mean"), sq[:, k, :], start=k == 0, stop=k == KD - 1)
                    i.then_inc(ph["yms"], 1)

                @block.scalar
                def _(act):
                    need(act, ph, xc=1)
                    act.activation(sq[:], xc[:], ACT.Square).then_inc(ph["sq"], 1)
                    need(act, ph, var_eps=1)
                    act.activation(r[:, 1, :], r[:, 0, :], ACT.Sqrt).then_inc(ph["sd"], 1)
                    need(act, ph, ms=1)
                    act.activation(r[:, 4, :], r[:, 3, :], ACT.Sqrt).then_inc(ph["sd1"], 1)
                    need(act, ph, xn=1)
                    act.activation(e_hi[:, :, ts], xn[:], ACT.Copy).then_inc(ph["xn_hi"], 1)
                    need(act, ph, h=KD)
                    act.activation(h_hi[:], h[:], ACT.Copy).then_inc(ph["h_hi"], 1)
                    need(act, ph, rank_ps=1)
                    act.activation(lowrank[:], bank[0:LR, 6, :], ACT.Copy).then_inc(ph["rank"], 1)
                    need(act, ph, v_ps=1)
                    act.activation(v[:].rearrange("p j d -> p (j d)"),
                                   bank[:, 0:2, :].rearrange("p j d -> p (j d)"), ACT.Copy).then_inc(ph["v"], 1)
                    need(act, ph, logits=1)
                    act.activation(rt["gate"][:], bank[:, 2, 0:NJ * 2 * E0]
                                   .rearrange("p (j e) -> p j e", j=NJ)[:, :, E0:2 * E0], ACT.Silu).then_inc(ph["rgate"], 1)
                    need(act, ph, shifted=1)
                    act.activation(rt["ex"][:, :, 0:E0], rt["sh"][:, :, 0:E0], ACT.Exp).then_inc(ph["rexp"], 1)
                    need(act, ph, gk_ps=1)
                    act.activation(gk, bank[:, 7, :], ACT.Abs, bias=col("gk_b")).then_inc(ph["absz"], 1)
                    need(act, ph, absz=1)
                    act.activation(e1, gk, ACT.Exp, scale=-1.0).then_inc(ph["e1"], 1)
                    need(act, ph, e1=1)
                    act.activation(l1, e1, ACT.Ln, bias=1.0).then_inc(ph["l1"], 1)
                    need(act, ph, cum=1)
                    act.activation(eb, cum, ACT.Exp, scale=1.0 / GNORM).then_inc(ph["eb"], 1)
                    act.activation(enb, cum, ACT.Exp, scale=-1.0 / GNORM).then_inc(ph["enb"], 1)
                    need(act, ph, rest=1)
                    act.activation(e1, mn, ACT.Exp, scale=1.0 / GNORM).then_inc(ph["el"], 1)
                    need(act, ph, cwt_ps=1)
                    act.activation(cw[:, ts], bank[:, 3, :], ACT.Copy).then_inc(ph["cw"], 1)
                    need(act, ph, gate_ps=1)
                    act.activation(sgate[:], bank[:, 2:4, :], ACT.Silu).then_inc(ph["sgate"], 1)
                    need(act, ph, klt_ps=1)
                    act.activation(klt[:].rearrange("p j k -> p (j k)"), bank[:, 6, :], ACT.Copy).then_inc(ph["klt"], 1)
                    need(act, ph, o_ps=NC0)
                    for gr in range(2):
                        act.activation(by_chunk(sq[:, gr, :]), heads_out(gr), ACT.Square).then_inc(ph["sqo"], 1)
                    need(act, ph, hms_eps=1)
                    act.activation(h[:], xc[:], ACT.Sqrt).then_inc(ph["hsd"], 1)
                    need(act, ph, og=1)
                    act.activation(og_hi[:], on[:], ACT.Copy).then_inc(ph["og_hi"], 1)
                    need(act, ph, y=1)
                    act.activation(sq[:], xc[:], ACT.Square).then_inc(ph["sqy"], 1)
                    need(act, ph, yms_eps=1)
                    act.activation(r[:, 1, :], r[:, 0, :], ACT.Sqrt).then_inc(ph["ysd"], 1)
                    need(act, ph, h2=KD)
                    act.activation(f_hi[:, :, ts], h[:], ACT.Copy).then_inc(ph["f_hi"], 1)

                @block.gpsimd
                def _(pool_):
                    need(pool_, ph, xn=1)
                    pool_.tensor_tensor(acc[:, :, ts], x[:], xn[:], ALU.add).then_inc(ph["acc"], 1)
                    need(pool_, ph, qe=1)
                    for c in range(NC0):
                        if c >= 2:
                            need(pool_, ph, a_ps=c - 1)
                        pool_.tensor_tensor(qb[:, c % 2], qe[:, c * CH:(c + 1) * CH].unsqueeze(1).broadcast_to([P, H0, CH]),
                                            col("headmask").unsqueeze(2).broadcast_to([P, H0, CH]), ALU.mult)\
                            .then_inc(ph["qb"], 1)

                @block.vector
                def _(dve):
                    need(dve, ph, mean=1)
                    dve.tensor_tensor(xc[:], x[:], both(bank[:, 0, :]), ALU.subtract).then_inc(ph["xc"], 1)
                    need(dve, ph, var=1)
                    dve.tensor_scalar_add(r[:, 0, :], bank[:, 1, :], 1e-5).then_inc(ph["var_eps"], 1)
                    need(dve, ph, sd=1)
                    dve.reciprocal(r[:, 5, :], r[:, 1, :]).then_inc(ph["rstd"], 1)
                    need(dve, ph, rstd=1)
                    dve.tensor_tensor(xn[:], xc[:], both(r[:, 5, :]), ALU.mult).then_inc(ph["xn"], 1)
                    dve.tensor_tensor(r[:, 2, :], bank[:, 1, :], r[:, 5, :], ALU.mult).then_inc(ph["vr"], 1)
                    need(dve, ph, vr=1)
                    dve.tensor_tensor(r[:, 3, :], r[:, 2, :], r[:, 5, :], ALU.mult).then_inc(ph["vrr"], 1)
                    need(dve, ph, vrr=1)
                    dve.tensor_scalar_add(r[:, 3, :], r[:, 3, :], 1e-6).then_inc(ph["ms"], 1)
                    need(dve, ph, sd1=1)
                    dve.reciprocal(r[:, 2, :], r[:, 4, :]).then_inc(ph["r1"], 1)
                    need(dve, ph, r1=1, xn=1)
                    for k in range(KD):
                        dve.scalar_tensor_tensor(h[:, k, :], xn[:, k, :], col("norm1")[:, k:k + 1], r[:, 2, :],
                                                 ALU.mult, ALU.mult).then_inc(ph["h"], 1)
                    need(dve, ph, xn_hi=1)
                    dve.tensor_tensor(e_lo[:, :, ts], xn[:], e_hi[:, :, ts].bitcast(F32), ALU.subtract).then_inc(ph["e_lo"], 1)
                    need(dve, ph, h_hi=1)
                    dve.tensor_tensor(h_lo[:], h[:], h_hi[:].bitcast(F32), ALU.subtract).then_inc(ph["h_lo"], 1)
                    need(dve, ph, rgate=1)
                    lg = bank[:, 2, 0:NJ * 2 * E0].rearrange("p (j e) -> p j e", j=NJ)
                    dve.tensor_tensor(rt["lg"][:, :, 0:E0], lg[:, :, 0:E0], rt["gate"][:], ALU.mult).then_inc(ph["lg"], 1)
                    need(dve, ph, lg=1)
                    dve.scalar_tensor_tensor(rt["lg"][:, :, 0:E0], rt["lg"][:, :, 0:E0], -1.0, rt["lg"][:, :, 0:E0],
                                             ALU.mult, ALU.max).then_inc(ph["lg"], 1)
                    need(dve, ph, lg=2)
                    softmax(dve, ph, rt, E0)
                    dve.tensor_tensor(rt["bi"][:, :, 0:E0], rt["pr"][:, :, 0:E0],
                                      col("bias0").unsqueeze(1).broadcast_to([P, NJ, E0]), ALU.add).then_inc(ph["biased"], 1)
                    need(dve, ph, biased=1)
                    top2(dve, ph, rt, "bi", E0, col("iota"))
                    dve.tensor_tensor(rt["sh"][:, :, 0:E0], rt["pr"][:, :, 0:E0],
                                      col("scale0").unsqueeze(1).broadcast_to([P, NJ, E0]), ALU.mult).then_inc(ph["scaled"], 1)
                    need(dve, ph, scaled=1)
                    dve.scalar_tensor_tensor(rt["ex"][:, :, 0:E0], rt["sh"][:, :, 0:E0], 1.0, rt["pick"][:, :, 0:E0],
                                             ALU.add, ALU.mult).then_inc(ph["comb"], 1)
                    dve.memset(rt["ex"][:, :, E0:NE], 1.0).then_inc(ph["comb"], 1)
                    need(dve, ph, comb=2)
                    for j in range(NJ):
                        dve.tensor_copy(rt["rep"][:, j], rt["ex"][:, j].unsqueeze(2).broadcast_to([P, NE, 8]))\
                            .then_inc(ph["rep"], 1)
                    need(dve, ph, absz=1)
                    dve.tensor_scalar(mn, bank[:, 7, :], col("gk_b"), 0.0, ALU.add, ALU.min).then_inc(ph["minz"], 1)
                    need(dve, ph, l1=1, minz=1)
                    dve.tensor_tensor(gs, mn, l1, ALU.subtract).then_inc(ph["gs"], 1)
                    need(dve, ph, gs=1)
                    dve.tensor_tensor_scan(cum, col("scan64"), gs, 0.0, ALU.mult, ALU.add).then_inc(ph["cum"], 1)
                    need(dve, ph, cum=1, minz=1)
                    c3 = cum.rearrange("p (c t) -> p c t", c=NC0)
                    dve.tensor_tensor(mn.rearrange("p (c t) -> p c t", c=NC0),
                                      c3[:, :, CH - 1:CH].broadcast_to([P, NC0, CH]), c3, ALU.subtract).then_inc(ph["rest"], 1)
                    need(dve, ph, eb=1, qk=1)
                    dve.scalar_tensor_tensor(qe[:], bank[:, 4, :], HK ** -0.5, eb, ALU.mult, ALU.mult).then_inc(ph["qe"], 1)
                    need(dve, ph, enb=1)
                    dve.tensor_tensor(ke[:], bank[:, 5, :], enb, ALU.mult).then_inc(ph["ke"], 1)
                    need(dve, ph, el=1)
                    dve.tensor_tensor(kl[:], bank[:, 5, :], e1, ALU.mult).then_inc(ph["kl"], 1)
                    for j in range(NJ):
                        need(dve, ph, a_ps=2 * j + 2)
                        if j >= 2:
                            need(dve, ph, o_ps=2 * j - 2)
                        dve.tensor_tensor(am[:, j % 2], bank[:, 4 + j % 2, :].rearrange("p (h c) -> p h c", h=H0),
                                          col("causal64").unsqueeze(1).broadcast_to([P, H0, CH]), ALU.mult)\
                            .then_inc(ph["am"], 1)
                        for u in range(2):
                            c = 2 * j + u
                            need(dve, ph, u_ps=c + 1)
                            if c >= 2:
                                need(dve, ph, state=c - 1)
                            dve.tensor_tensor(um[:, u], bank[:, 6 + u, 0:D], col("bdmask"), ALU.mult).then_inc(ph["um"], 1)
                            need(dve, ph, um=c + 1)
                            if c:
                                need(dve, ph, o_ps=c, state=c)
                            dve.scalar_tensor_tensor(state[:, (c + 1) % 2], state[:, c % 2],
                                                     eb[:, (c + 1) * CH - 1:(c + 1) * CH], um[:, u],
                                                     ALU.mult, ALU.add).then_inc(ph["state"], 1)
                    need(dve, ph, hms=1, sqo=2)
                    dve.tensor_scalar_add(xc[:], bank[:, 4:6, :], 1e-6).then_inc(ph["hms_eps"], 1)
                    need(dve, ph, hsd=1)
                    dve.reciprocal(on[:], h[:]).then_inc(ph["hr"], 1)
                    need(dve, ph, hr=1)
                    for gr in range(2):
                        dve.tensor_tensor(by_chunk(xc[:, gr, :]), heads_out(gr), by_chunk(on[:, gr, :]), ALU.mult)\
                            .then_inc(ph["onorm"], 1)
                    need(dve, ph, onorm=2, sgate=1)
                    dve.scalar_tensor_tensor(on[:], xc[:], col("gnorm"), sgate[:], ALU.mult, ALU.mult).then_inc(ph["og"], 1)
                    need(dve, ph, og_hi=1)
                    dve.tensor_tensor(og_lo[:], on[:], og_hi[:].bitcast(F32), ALU.subtract).then_inc(ph["og_lo"], 1)
                    need(dve, ph, gla_ps=1, acc=1)
                    dve.tensor_tensor(acc[:, :, ts], bank[:, 2:4, :], acc[:, :, ts], ALU.add).then_inc(ph["acc"], 1)
                    dve.tensor_tensor(xc[:], bank[:, 2:4, :], xn[:], ALU.add).then_inc(ph["y"], 1)
                    need(dve, ph, yms=1)
                    dve.tensor_scalar_add(r[:, 0, :], bank[:, 6, :], 1e-6).then_inc(ph["yms_eps"], 1)
                    need(dve, ph, ysd=1)
                    dve.reciprocal(r[:, 2, :], r[:, 1, :]).then_inc(ph["r2"], 1)
                    need(dve, ph, r2=1, y=1, hr=1)
                    for k in range(KD):
                        dve.scalar_tensor_tensor(h[:, k, :], xc[:, k, :], col("ffn_norm")[:, k:k + 1], r[:, 2, :],
                                                 ALU.mult, ALU.mult).then_inc(ph["h2"], 1)
                    need(dve, ph, f_hi=1)
                    dve.tensor_tensor(f_lo[:, :, ts], h[:], f_hi[:, :, ts].bitcast(F32), ALU.subtract)
            ph.clear()


def router_tiles(sb, tag):
    t = {n: sb(tag + n, [P, NJ, NE]) for n in ("lg", "sh", "ex", "pr", "bi", "pick", "one")}
    t["gate"] = sb(tag + "gate", [P, NJ, E0])
    t["m"] = sb(tag + "m", [P, NJ, 4])
    t["top"] = sb(tag + "top", [P, NJ, 8])
    t["idx"] = sb(tag + "idx", [P, NJ, 8], U32)
    t["idf"] = sb(tag + "idf", [P, NJ, 8])
    t["rep"] = sb(tag + "rep", [P, NJ, NE, 8])
    return t


def router_logits(pe, ph, bank, xn, w, n):
    for j in range(NJ):
        for k in range(KD):
            i = pe.matmul(bank[:, 2, j * n:(j + 1) * n], xn[:, k, j * P:(j + 1) * P], w[:, k, :],
                          start=k == 0, stop=k == KD - 1)
    i.then_inc(ph["logits"], 1)


def router_transpose(pe, ph, bank, rt, ident):
    need(pe, ph, rep=NJ)
    for j in range(NJ):
        i = pe.transpose(bank[:, 3, j * P:(j + 1) * P], rt["rep"][:, j].rearrange("p e r -> p (e r)"), ident)
    i.then_inc(ph["cwt_ps"], 1)


def softmax(dve, ph, rt, n):
    def wide(a):
        return a.broadcast_to([P, NJ, n])
    dve.tensor_reduce(rt["m"][:, :, 0:1], rt["lg"][:, :, 0:n], AX.X, ALU.max).then_inc(ph["rmax"], 1)
    need(dve, ph, rmax=1)
    dve.tensor_tensor(rt["sh"][:, :, 0:n], rt["lg"][:, :, 0:n], wide(rt["m"][:, :, 0:1]), ALU.subtract)\
        .then_inc(ph["shifted"], 1)
    need(dve, ph, rexp=1)
    dve.tensor_reduce(rt["m"][:, :, 1:2], rt["ex"][:, :, 0:n], AX.X, ALU.add).then_inc(ph["rsum"], 1)
    need(dve, ph, rsum=1)
    dve.reciprocal(rt["m"][:, :, 2:3], rt["m"][:, :, 1:2]).then_inc(ph["rrec"], 1)
    need(dve, ph, rrec=1)
    dve.tensor_tensor(rt["pr"][:, :, 0:n], rt["ex"][:, :, 0:n], wide(rt["m"][:, :, 2:3]), ALU.mult)\
        .then_inc(ph["prob"], 1)
    need(dve, ph, prob=1)


def top2(dve, ph, rt, src, n, iota):
    for j in range(NJ):
        dve.max(rt["top"][:, j, :], rt[src][:, j, 0:n]).then_inc(ph["top"], 1)
    need(dve, ph, top=NJ)
    for j in range(NJ):
        dve.max_index(rt["idx"][:, j, :], rt["top"][:, j, :], rt[src][:, j, 0:n]).then_inc(ph["idx"], 1)
    need(dve, ph, idx=NJ)
    dve.tensor_copy(rt["idf"][:], rt["idx"][:]).then_inc(ph["idf"], 1)
    need(dve, ph, idf=1)
    io = iota[:, 0:n].unsqueeze(1).broadcast_to([P, NJ, n])
    dve.tensor_tensor(rt["one"][:, :, 0:n], io, rt["idf"][:, :, 0:1].broadcast_to([P, NJ, n]), ALU.is_equal)\
        .then_inc(ph["hot"], 1)
    dve.tensor_tensor(rt["pick"][:, :, 0:n], io, rt["idf"][:, :, 1:2].broadcast_to([P, NJ, n]), ALU.is_equal)\
        .then_inc(ph["hot"], 1)
    need(dve, ph, hot=2)
    dve.tensor_tensor(rt["pick"][:, :, 0:n], rt["pick"][:, :, 0:n], rt["one"][:, :, 0:n], ALU.add)\
        .then_inc(ph["pick"], 1)
    need(dve, ph, pick=1)


def mlp(nc, pool, bank, name, w_dram, x_hi, x_lo, cw, acc):
    pairs = w_dram.shape[0] // 2
    UN = 2 * NS
    with ExitStack() as own:
        def sb(n, shape, dt=F32):
            return own.enter_context(nc.sbuf_tensor(name + n, shape, dt))

        raw = sb("_raw", [P, 2, MLP_W])
        w_hi, w_lo = sb("_whi", [P, 2, MLP_W], F32R), sb("_wlo", [P, 2, MLP_W], F32R)
        sg = sb("_sg", [P, 2, TS])
        su = sb("_su", [P, 2, TS])
        hh = sb("_h", [P, 2, TS]) if cw is not None else su
        h_hi, h_lo = sb("_hhi", [P, 2, TS], F32R), sb("_hlo", [P, 2, TS], F32R)
        ph = Phase(nc, pool)
        SU, LO, H, DOWN, ADDED, SPLIT = 2, 2, 2, 2, 2, 1

        def half(t, j, a):
            return t[:, j, a:a + P]

        def bodies(eng, emit):
            emit(0, True, pairs == 1)
            if pairs > 2:
                with eng.Fori(1, pairs - 1) as i:
                    emit(i, False, False)
            if pairs > 1:
                emit(pairs - 1, False, True)

        with nc.Block(no_gpsimd_drain=True) as block:

            @block.sync
            def _(sp):
                def emit(i, first, last):
                    for j in range(2):
                        sp.wait_ge(ph[f"split{j}"], i + SPLIT)
                        src = w_dram[bass.ds(i * 2 + j, 1)].rearrange("o p c -> (o p) c")
                        sp.dma_start(raw[:, j, :], src).then_inc(ph[f"raw{j}"], 16)
                sp.sem_inc(ph["split0"], SPLIT)
                sp.sem_inc(ph["split1"], SPLIT)
                bodies(sp, emit)
                sp.wait_ge(ph["raw0"], 16 * pairs)
                sp.wait_ge(ph["raw1"], 16 * pairs)

            @block.tensor
            def _(pe):
                def gate_and_up(j, c, n):
                    pe.wait_ge(ph["su"], n - 2 + 1 + SU)
                    for m in range(2):
                        for k in range(KD):
                            a = (2 * k + m) * P
                            i = mm3(pe, bank[:, 2 * (c % 2) + m, :], (half(w_hi, j, a), half(w_lo, j, a)),
                                    (x_hi[:, k, c * TS:(c + 1) * TS], x_lo[:, k, c * TS:(c + 1) * TS]),
                                    k == 0, k == KD - 1)
                    i.then_inc(ph["gu"], 1)

                def emit(i, first, last):
                    for u in range(UN):
                        n = i * UN + u
                        if u + 1 == NS:
                            pe.wait_ge(ph["split1"], i + 1 + SPLIT)
                        if u + 1 < UN:
                            gate_and_up((u + 1) // NS, (u + 1) % NS, n + 1)
                        elif not last:
                            pe.wait_ge(ph["split0"], i + 2 + SPLIT)
                            gate_and_up(0, 0, n + 1)
                        pe.wait_ge(ph["lo"], n + 1 + LO)
                        pe.wait_ge(ph["added"], n - 2 + 1 + ADDED)
                        for m in range(KD):
                            a = 2 * KD * P + m * P
                            q = mm3(pe, bank[:, 4 + 2 * (u % 2) + m, :], (half(w_hi, u // NS, a), half(w_lo, u // NS, a)),
                                    (h_hi[:, u % 2, :], h_lo[:, u % 2, :]))
                        q.then_inc(ph["down"], 1)
                pe.sem_inc(ph["down"], DOWN)
                pe.wait_ge(ph["split0"], 1 + SPLIT)
                gate_and_up(0, 0, 0)
                bodies(pe, emit)

            @block.scalar
            def _(act):
                def split_high(j, k, done):
                    act.wait_ge(ph[f"raw{j}"], k * 16 + 16)
                    act.wait_ge(ph["down"], done + DOWN)
                    act.activation(w_hi[:, j, :], raw[:, j, :], ACT.Copy).then_inc(ph[f"high{j}"], 1)

                def emit(i, first, last):
                    for u in range(UN):
                        n = i * UN + u
                        c = u % 2
                        act.wait_ge(ph["gu"], n + 1)
                        act.wait_ge(ph["su"], n - 2 + 1 + SU)
                        act.activation(sg[:, c, :], bank[:, 2 * c, :], ACT.Silu).then_inc(ph["silu"], 1)
                        if u == 1:
                            split_high(1, i, i * UN)
                        if u == NS + 1 and not last:
                            split_high(0, i + 1, i * UN + NS)
                        if cw is None:
                            act.wait_ge(ph["su"], n + 1 + SU)
                        else:
                            act.wait_ge(ph["h"], n + 1 + H)
                        act.wait_ge(ph["down"], n - 2 + 1 + DOWN)
                        act.activation(h_hi[:, c, :], hh[:, c, :], ACT.Copy).then_inc(ph["hi"], 1)
                split_high(0, 0, 0)
                bodies(act, emit)

            @block.gpsimd
            def _(pl):
                def emit(i, first, last):
                    for u in range(UN):
                        n = i * UN + u
                        c = u % 2
                        pl.wait_ge(ph["su"], n + 1 + SU)
                        pl.wait_ge(ph["lo"], n - 2 + 1 + LO)
                        pl.tensor_tensor(hh[:, c, :], su[:, c, :], cw[:, (u % NS) * TS:(u % NS + 1) * TS], ALU.mult)\
                            .then_inc(ph["h"], 1)
                if cw is not None:
                    pl.sem_inc(ph["h"], H)
                    bodies(pl, emit)

            @block.vector
            def _(dve):
                def split_low(j, k):
                    dve.wait_ge(ph[f"high{j}"], k + 1)
                    dve.tensor_tensor(w_lo[:, j, :], raw[:, j, :], w_hi[:, j, :].bitcast(F32), ALU.subtract)\
                        .then_inc(ph[f"split{j}"], 1)

                def add(c, n):
                    dve.wait_ge(ph["down"], n + 1 + DOWN)
                    dve.wait_ge(ph["added"], n - 1 + ADDED)
                    s = acc[:, :, c * TS:(c + 1) * TS]
                    dve.tensor_tensor(s, bank[:, 4 + 2 * (c % 2):6 + 2 * (c % 2), :], s, ALU.add).then_inc(ph["added"], 1)

                def emit(i, first, last):
                    for u in range(UN):
                        n = i * UN + u
                        c = u % 2
                        dve.wait_ge(ph["silu"], n + 1)
                        if cw is None:
                            dve.wait_ge(ph["lo"], n - 2 + 1 + LO)
                        else:
                            dve.wait_ge(ph["h"], n - 2 + 1 + H)
                        dve.tensor_tensor(su[:, c, :], bank[:, 2 * c + 1, :], sg[:, c, :], ALU.mult).then_inc(ph["su"], 1)
                        if u == 1:
                            split_low(1, i)
                        if u == NS + 1 and not last:
                            split_low(0, i + 1)
                        if not (first and u == 0):
                            add((u + NS - 1) % NS, n - 1)
                        dve.wait_ge(ph["hi"], n + 1)
                        dve.tensor_tensor(h_lo[:, c, :], hh[:, c, :], h_hi[:, c, :].bitcast(F32), ALU.subtract)\
                            .then_inc(ph["lo"], 1)
                dve.sem_inc(ph["su"], SU)
                dve.sem_inc(ph["lo"], LO)
                dve.sem_inc(ph["added"], ADDED)
                split_low(0, 0)
                bodies(dve, emit)
                add(NS - 1, pairs * UN - 1)
        ph.clear()


def ssm_prepare(nc, pool, bank, wbc, a_dram, acc, e_hi, e_lo, f_hi, f_lo, cw, st, col, colk):
    with ExitStack() as own:
        def sb(name, shape, dt=F32):
            return own.enter_context(nc.sbuf_tensor(name, shape, dt))

        w_raw = sb("bc_raw", [P, KD, D])
        w_hi, w_lo = sb("bc_hi", [P, KD, D], F32R), sb("bc_lo", [P, KD, D], F32R)
        neg_a = sb("neg_a", [HM, 2])
        ph = Phase(nc, pool)
        with nc.Block(no_gpsimd_drain=True) as block:
            @block.sync
            def _(sp):
                sp.dma_start(w_raw[:], wbc).then_inc(ph["raw"], 16)
                sp.wait_ge(ph["raw"], 16)

            @block.scalar
            def _(act):
                act.activation(neg_a[:, 0:1], col("A_log")[0:HM], ACT.Exp).then_inc(ph["exp"], 1)

            @block.vector
            def _(dve):
                need(dve, ph, exp=1)
                dve.tensor_scalar_mul(neg_a[:, 1:2], neg_a[:, 0:1], -1.0)
                need(dve, ph, raw=16)
                dve.tensor_copy(w_hi[:], w_raw[:]).then_inc(ph["hi"], 1)
                need(dve, ph, hi=1)
                dve.tensor_tensor(w_lo[:], w_raw[:], w_hi[:].bitcast(F32), ALU.subtract)
        ph.clear()

        xc, sq = sb("pxc", [P, KD, TS]), sb("psq", [P, KD, TS])
        r = sb("pr", [P, 6, TS])
        xn, hm = sb("pxn", [P, KD, TS]), sb("phm", [P, KD, TS])
        rt = router_tiles(sb, "rt1_")
        b_feat = sb("b_feat", [P, TS])
        q = sb("dt_q", [HM, 12, TS])

        def both(a):
            return a.unsqueeze(1).broadcast_to([P, KD, TS])

        with nc.Fori(0, NS) as s:
            ph = Phase(nc, pool)
            ts = bass.ds(s * TS, TS)
            js4 = bass.ds(s * NJ, NJ)
            absz, ez, u, lnu, d, c, ru, mx, dt, adt, a, rest = (q[:, i, :] for i in range(12))
            with nc.Block(no_gpsimd_drain=True) as block:

                @block.sync
                def _(sp):
                    need(sp, ph, a=1)
                    sp.dma_start(a_dram[:, ts], a).then_inc(ph["a_out"], 16)
                    need(sp, ph, a_out=16)

                @block.tensor
                def _(pe):
                    for k in range(KD):
                        i = pe.matmul(bank[:, 0, :], col("mean"), acc[:, k, ts], start=k == 0, stop=k == KD - 1)
                    i.then_inc(ph["mean"], 1)
                    need(pe, ph, sq=1)
                    for k in range(KD):
                        i = pe.matmul(bank[:, 1, :], col("mean"), sq[:, k, :], start=k == 0, stop=k == KD - 1)
                    i.then_inc(ph["var"], 1)
                    need(pe, ph, xn=1)
                    router_logits(pe, ph, bank, xn, colk("router1"), NE)
                    need(pe, ph, hm=KD)
                    for k in range(KD):
                        i = pe.matmul(bank[0:HM, 6, :], colk("wdt")[:, k, :], hm[:, k, :], start=k == 0, stop=k == KD - 1)
                    i.then_inc(ph["dt_ps"], 1)
                    need(pe, ph, f_hi=1, f_lo=1)
                    for m in range(2):
                        for k in range(KD):
                            cs = slice(m * P, m * P + P)
                            i = mm3(pe, bank[:, 4 + m, :], (w_hi[:, k, cs], w_lo[:, k, cs]),
                                    (f_hi[:, k, ts], f_lo[:, k, ts]), k == 0, k == KD - 1)
                    i.then_inc(ph["bc_ps"], 1)
                    need(pe, ph, b_feat=1)
                    for j in range(NJ):
                        i = pe.transpose(bank[:, 7, j * P:(j + 1) * P], b_feat[:, j * P:(j + 1) * P], col("ident"))
                    i.then_inc(ph["bt_ps"], 1)
                    need(pe, ph, c_feat=1)
                    for j in range(NJ):
                        i = pe.matmul(bank[:, 4, j * P:(j + 1) * P], b_feat[:, j * P:(j + 1) * P],
                                      st["c_feat"][:, bass.ds(s * TS + j * P, P)], start=True, stop=True)
                    i.then_inc(ph["cb_ps"], 1)
                    router_transpose(pe, ph, bank, rt, col("ident"))
                    need(pe, ph, a=1, wend=1)
                    for m, src in ((0, a), (1, rest)):
                        for j in range(NJ):
                            o = (m * NJ + j) * HM
                            i = pe.transpose(bank[:, 6, o:o + HM], src[:, j * P:(j + 1) * P], col("ident")[0:HM, 0:HM])
                    i.then_inc(ph["at_ps"], 1)

                @block.scalar
                def _(act):
                    need(act, ph, xc=1)
                    act.activation(sq[:], xc[:], ACT.Square).then_inc(ph["sq"], 1)
                    need(act, ph, var_eps=1)
                    act.activation(r[:, 1, :], r[:, 0, :], ACT.Sqrt).then_inc(ph["sd"], 1)
                    need(act, ph, ms=1)
                    act.activation(r[:, 4, :], r[:, 3, :], ACT.Sqrt).then_inc(ph["sd1"], 1)
                    need(act, ph, xn=1)
                    act.activation(e_hi[:, :, ts], xn[:], ACT.Copy).then_inc(ph["xn_hi"], 1)
                    need(act, ph, hm=KD)
                    act.activation(f_hi[:, :, ts], hm[:], ACT.Copy).then_inc(ph["f_hi"], 1)
                    need(act, ph, shifted=1)
                    act.activation(rt["ex"][:], rt["sh"][:], ACT.Exp).then_inc(ph["rexp"], 1)
                    need(act, ph, dt_ps=1)
                    act.activation(absz, bank[0:HM, 6, :], ACT.Abs, bias=col("dt_bias")[0:HM]).then_inc(ph["absz"], 1)
                    need(act, ph, absz=1)
                    act.activation(ez, absz, ACT.Exp, scale=-1.0).then_inc(ph["ez"], 1)
                    need(act, ph, u=1)
                    act.activation(lnu, u, ACT.Ln).then_inc(ph["lnu"], 1)
                    need(act, ph, bc_ps=1)
                    act.activation(b_feat[:], bank[:, 4, :], ACT.Copy).then_inc(ph["b_feat"], 1)
                    act.activation(st["c_feat"][:, ts], bank[:, 5, :], ACT.Copy).then_inc(ph["c_feat"], 1)
                    need(act, ph, bt_ps=1)
                    act.activation(st["b_tok"][:, js4, :].rearrange("p j n -> p (j n)"), bank[:, 7, :], ACT.Copy)
                    need(act, ph, rest=1)
                    act.activation(rest, rest, ACT.Exp).then_inc(ph["wend"], 1)
                    need(act, ph, cwt_ps=1)
                    act.activation(cw[:, ts], bank[:, 3, :], ACT.Copy)
                    need(act, ph, at_ps=1)
                    for m, n in ((0, "a_tok"), (1, "w_tok")):
                        act.activation(st[n][:, js4, :].rearrange("p j h -> p (j h)"),
                                       bank[:, 6, m * NJ * HM:(m + 1) * NJ * HM], ACT.Copy)

                @block.gpsimd
                def _(pl):
                    need(pl, ph, xn=1)
                    pl.tensor_tensor(acc[:, :, ts], acc[:, :, ts], xn[:], ALU.add).then_inc(ph["acc"], 1)
                    need(pl, ph, acc=1)

                @block.vector
                def _(dve):
                    need(dve, ph, mean=1)
                    dve.tensor_tensor(xc[:], acc[:, :, ts], both(bank[:, 0, :]), ALU.subtract).then_inc(ph["xc"], 1)
                    need(dve, ph, var=1)
                    dve.tensor_scalar_add(r[:, 0, :], bank[:, 1, :], 1e-5).then_inc(ph["var_eps"], 1)
                    need(dve, ph, sd=1)
                    dve.reciprocal(r[:, 5, :], r[:, 1, :]).then_inc(ph["rstd"], 1)
                    need(dve, ph, rstd=1)
                    dve.tensor_tensor(xn[:], xc[:], both(r[:, 5, :]), ALU.mult).then_inc(ph["xn"], 1)
                    dve.tensor_tensor(r[:, 2, :], bank[:, 1, :], r[:, 5, :], ALU.mult).then_inc(ph["vr"], 1)
                    need(dve, ph, vr=1)
                    dve.tensor_tensor(r[:, 3, :], r[:, 2, :], r[:, 5, :], ALU.mult).then_inc(ph["vrr"], 1)
                    need(dve, ph, vrr=1)
                    dve.tensor_scalar_add(r[:, 3, :], r[:, 3, :], 1e-5).then_inc(ph["ms"], 1)
                    need(dve, ph, sd1=1)
                    dve.reciprocal(r[:, 2, :], r[:, 4, :]).then_inc(ph["r1"], 1)
                    need(dve, ph, r1=1, xn=1)
                    for k in range(KD):
                        dve.scalar_tensor_tensor(hm[:, k, :], xn[:, k, :], col("norm_m")[:, k:k + 1], r[:, 2, :],
                                                 ALU.mult, ALU.mult).then_inc(ph["hm"], 1)
                    need(dve, ph, xn_hi=1)
                    dve.tensor_tensor(e_lo[:, :, ts], xn[:], e_hi[:, :, ts].bitcast(F32), ALU.subtract)
                    need(dve, ph, f_hi=1)
                    dve.tensor_tensor(f_lo[:, :, ts], hm[:], f_hi[:, :, ts].bitcast(F32), ALU.subtract).then_inc(ph["f_lo"], 1)
                    need(dve, ph, logits=1)
                    dve.tensor_copy(rt["lg"][:], bank[:, 2, 0:NJ * NE].rearrange("p (j e) -> p j e", j=NJ)).then_inc(ph["lg"], 1)
                    need(dve, ph, lg=1)
                    softmax(dve, ph, rt, NE)
                    top2(dve, ph, rt, "pr", NE, col("iota"))
                    dve.tensor_tensor(rt["m"][:, :, 3:4], rt["top"][:, :, 0:1], rt["top"][:, :, 1:2], ALU.add)\
                        .then_inc(ph["topsum"], 1)
                    need(dve, ph, topsum=1)
                    dve.reciprocal(rt["m"][:, :, 0:1], rt["m"][:, :, 3:4]).then_inc(ph["toprec"], 1)
                    need(dve, ph, toprec=1)
                    dve.tensor_tensor(rt["sh"][:], rt["pr"][:], rt["m"][:, :, 0:1].broadcast_to([P, NJ, NE]), ALU.mult)\
                        .then_inc(ph["scaled"], 1)
                    need(dve, ph, scaled=1)
                    dve.tensor_tensor(rt["ex"][:], rt["sh"][:], rt["pick"][:], ALU.mult).then_inc(ph["comb"], 1)
                    need(dve, ph, comb=1)
                    for j in range(NJ):
                        dve.tensor_copy(rt["rep"][:, j], rt["ex"][:, j].unsqueeze(2).broadcast_to([P, NE, 8]))\
                            .then_inc(ph["rep"], 1)
                    need(dve, ph, ez=1)
                    dve.tensor_scalar_add(u, ez, 1.0).then_inc(ph["u"], 1)
                    dve.tensor_scalar(mx, bank[0:HM, 6, :], col("dt_bias")[0:HM], 0.0, ALU.add, ALU.max).then_inc(ph["mx"], 1)
                    need(dve, ph, u=1)
                    dve.tensor_scalar_add(d, u, -1.0).then_inc(ph["d"], 1)
                    dve.reciprocal(ru, u).then_inc(ph["ru"], 1)
                    need(dve, ph, d=1, ru=1)
                    dve.tensor_tensor(c, ez, d, ALU.subtract).then_inc(ph["c"], 1)
                    need(dve, ph, c=1)
                    dve.tensor_tensor(d, c, ru, ALU.mult).then_inc(ph["cr"], 1)
                    need(dve, ph, cr=1, lnu=1)
                    dve.tensor_tensor(dt, lnu, d, ALU.add).then_inc(ph["sp"], 1)
                    need(dve, ph, sp=1, mx=1)
                    dve.tensor_tensor(dt, dt, mx, ALU.add).then_inc(ph["dt"], 1)
                    need(dve, ph, dt=1)
                    dve.tensor_scalar_mul(adt, dt, neg_a[:, 1:2]).then_inc(ph["adt"], 1)
                    need(dve, ph, adt=1)
                    dve.tensor_tensor_scan(a, col("scan128")[0:HM], adt, 0.0, ALU.mult, ALU.add).then_inc(ph["a"], 1)
                    need(dve, ph, a=1)
                    a3 = a.rearrange("p (j t) -> p j t", j=NJ)
                    dve.tensor_tensor(rest.rearrange("p (j t) -> p j t", j=NJ),
                                      a3[:, :, P - 1:P].broadcast_to([HM, NJ, P]), a3, ALU.subtract).then_inc(ph["rest"], 1)
                    need(dve, ph, cb_ps=1)
                    dve.tensor_tensor(st["cb"][:, js4, :], bank[:, 4, :].rearrange("p (j t) -> p j t", j=NJ),
                                      col("causal128").unsqueeze(1).broadcast_to([P, NJ, P]), ALU.mult)
            ph.clear()


def ssm(nc, pool, bank, m_dram, a_dram, acc, f_hi, f_lo, st, col):
    with ExitStack() as own:
        def sb(name, shape, dt=F32):
            return own.enter_context(nc.sbuf_tensor(name, shape, dt))

        b_tok, c_feat, cb, a_tok, w_tok = (st[n] for n in ("b_tok", "c_feat", "cb", "a_tok", "w_tok"))
        proj = sb("proj", [P, KD, T])
        y2 = sb("y2", [P, T])
        a_wide = sb("a_wide", [P, 2, T])
        a_feat = sb("a_feat", [P, T])
        raw = sb("m_raw", [P, MP_W])
        wi_hi, wi_lo = sb("wi_hi", [P, MP_IN], F32R), sb("wi_lo", [P, MP_IN], F32R)
        wo_s = sb("wo_s", [P, MP_OUT])
        wo_hi, wo_lo = sb("wo_hi", [P, MP_OUT], F32R), sb("wo_lo", [P, MP_OUT], F32R)
        taps = sb("taps", [P, 8])
        prev = sb("prev", [P, 4])
        skip = sb("skip", [P, 1])
        s_init = sb("s_init", [P, P])
        xbuf = sb("xbuf", [P, 2, NR - 1 + TS])
        cv, th = sb("cv", [P, TS]), sb("th", [P, TS])
        xs = sb("xs", [P, 2, TS])
        tz = sb("tz", [P, TS])
        zs = sb("zs", [P, 2, TS])
        x_tok = sb("x_tok", [P, NJ, P])
        xd = sb("xd", [P, NJ, P])
        a_here, w_here = sb("a_here", [P, T // P, 2]), sb("w_here", [P, T // P, 2])
        mt = sb("mt", [P, 2, TS])
        mm = sb("mm", [P, 2, TS])
        dec = sb("dec", [P, 2, 2, NJ])
        state = sb("state_m", [P, 2, NJ, P])
        ea = sb("ea", [P, TS])
        t1, t2, y, ys = sb("t1", [P, TS]), sb("t2", [P, TS]), sb("y", [P, TS]), sb("ys", [P, TS])
        yz = sb("yz", [P, TS])
        yz_hi, yz_lo = sb("yz_hi", [P, TS], F32R), sb("yz_lo", [P, TS], F32R)

        ph = Phase(nc, pool)
        CR = {"xb": 1, "c0": 1, "zs": 1, "xs": 1, "xd": 1, "u": 1, "state": NJ + 1, "mm": 1, "ip": 1, "intra": 1, "inter": 1,
              "t1": 1, "t2": 2, "y": 1, "ys": 1, "yz": 2, "y2": 1, "lo": 1, "out": 1, "added": 1, "skip": 1,
              "wo_lo": 1, "ea": 1, "arg": 1}
        OWNER = {"xb": "scalar", "c0": "scalar", "zs": "vector", "xs": "vector", "xd": "vector", "u": "tensor", "state": "vector",
                 "mm": "gpsimd", "ip": "tensor", "intra": "tensor", "inter": "tensor", "t1": "vector",
                 "t2": "vector", "y": "gpsimd", "ys": "scalar", "yz": "gpsimd", "lo": "vector",
                 "out": "tensor", "skip": "scalar", "wo_lo": "vector", "ea": "scalar", "arg": "vector"}

        def credit(eng, who):
            for n, o in OWNER.items():
                if o == who:
                    eng.sem_inc(ph[n], CR[n])

        def done(eng, name, g, per=1):
            eng.wait_ge(ph[name], (g + 1) * per + CR.get(name, 0))

        def tiles(eng, emit):
            emit(0, True, False)
            with eng.Fori(1, NCT - 1) as t:
                emit(t, False, False)
            emit(NCT - 1, False, True)

        def step(s):
            return slice(s * TS, (s + 1) * TS)

        with nc.Block(no_gpsimd_drain=True) as block:

            @block.sync
            def _(sp):
                def load_raw(t):
                    sp.dma_start(raw[:], m_dram[bass.ds(t, 1)].rearrange("o p c -> (o p) c")).then_inc(ph["raw"], 16)

                def load_wide(t, s):
                    src = a_dram[bass.ds(t * 2, 2), step(s)]
                    sp.dma_start(a_wide[:, :, step(s)], src.partition_broadcast(P)).then_inc(ph[f"wide{s}"], 16)

                def load_feat(t, s):
                    for h in range(2):
                        src = a_dram[bass.ds(t * 2 + h, 1), step(s)].rearrange("o t -> (o t)")
                        sp.dma_start(a_feat[h * PH:(h + 1) * PH, step(s)], src.partition_broadcast(PH))\
                            .then_inc(ph[f"feat{s}"], 16)

                def emit(t, first, last):
                    done(sp, "wo_lo", t)
                    if not last:
                        load_raw(t + 1)
                        for s in range(NS):
                            g = t * NS + s
                            done(sp, "dec", g)
                            load_wide(t + 1, s)
                            done(sp, "ea", g)
                            load_feat(t + 1, s)
                load_raw(0)
                for s in range(NS):
                    load_wide(0, s)
                    load_feat(0, s)
                tiles(sp, emit)
                for s in range(NS):
                    sp.wait_ge(ph[f"wide{s}"], 16 * NCT)
                    sp.wait_ge(ph[f"feat{s}"], 32 * NCT)

            @block.tensor
            def _(pe):
                def project_in(g, s):
                    done(pe, "c0", g - 1)
                    done(pe, "zs", g - 1)
                    for m in range(2):
                        for k in range(KD):
                            a = slice((2 * k + m) * P, (2 * k + m) * P + P)
                            i = mm3(pe, bank[:, m, :], (wi_hi[:, a], wi_lo[:, a]),
                                    (f_hi[:, k, step(s)], f_lo[:, k, step(s)]), k == 0, k == KD - 1)
                    i.then_inc(ph["ip"], 1)

                def turn(g, s):
                    done(pe, "xs", g)
                    done(pe, "xd", g - 1)
                    for j in range(NJ):
                        i = pe.transpose(bank[:, 2, j * P:(j + 1) * P], xs[:, s % 2, j * P:(j + 1) * P], col("ident"))
                    i.then_inc(ph["xt"], 1)

                def update(g, s):
                    done(pe, "xd", g)
                    done(pe, "state", g - 1, NJ)
                    for j in range(NJ):
                        i = pe.matmul(bank[:, 5, j * P:(j + 1) * P], b_tok[:, s * NJ + j, :], xd[:, j, :],
                                      start=True, stop=True)
                    i.then_inc(ph["u"], 1)

                def scores(g, s):
                    done(pe, "mm", g)
                    done(pe, "x_tok", g)
                    done(pe, "t2", g - 1)
                    for j in range(NJ):
                        for h in range(2):
                            i = pe.matmul(bank[h * PH:(h + 1) * PH, 3, j * P:(j + 1) * P],
                                          x_tok[:, j, h * PH:(h + 1) * PH], mm[:, h, j * P:(j + 1) * P], start=True, stop=True)
                    i.then_inc(ph["intra"], 1)

                def from_state(g, s):
                    done(pe, "state", g, NJ)
                    done(pe, "t1", g - 1)
                    for j in range(NJ):
                        if j:
                            before = state[:, s % 2, j - 1, :]
                        else:
                            before = state[:, 1 - s % 2, NJ - 1, :] if s else s_init[:]
                        a = s * TS + j * P
                        i = pe.matmul(bank[:, 4, j * P:(j + 1) * P], before, c_feat[:, a:a + P], start=True, stop=True)
                    i.then_inc(ph["inter"], 1)

                def project_out(g):
                    done(pe, "lo", g)
                    done(pe, "added", g - 1)
                    for m in range(KD):
                        a = slice(m * P, (m + 1) * P)
                        i = mm3(pe, bank[:, 6 + m, :], (wo_hi[:, a], wo_lo[:, a]), (yz_hi[:], yz_lo[:]))
                    i.then_inc(ph["out"], 1)

                def emit(t, first, last):
                    for s in range(NS):
                        g = t * NS + s
                        n = (s + 1) % NS
                        more = not (last and s == NS - 1)
                        if s == NS - 1 and more:
                            done(pe, "wi_lo", t + 1)
                        if more:
                            project_in(g + 1, n)
                        update(g, s)
                        scores(g, s)
                        from_state(g, s)
                        if not (first and s == 0):
                            if s == 1:
                                done(pe, "wo_lo", t)
                            project_out(g - 1)
                        if more:
                            turn(g + 1, n)
                credit(pe, "tensor")
                done(pe, "wi_lo", 0)
                project_in(0, 0)
                turn(0, 0)
                tiles(pe, emit)
                project_out(NCT * NS - 1)
                done(pe, "y2", NCT * NS - 1)
                for s in range(NS):
                    i = pe.matmul(bank[:, s, :], col("mean_di"), y2[:, step(s)], start=True, stop=True)
                i.then_inc(ph["yms"], 1)

            @block.scalar
            def _(act):
                def take_weights(t):
                    act.wait_ge(ph["raw"], t * 16 + 16)
                    done(act, "ip", t * NS - 1)
                    act.activation(wi_hi[:], raw[:, 0:MP_IN], ACT.Copy).then_inc(ph["wi_hi"], 1)

                def take_vectors(t, head):
                    if not head:
                        done(act, "inter", t * NS - NS)
                    act.activation(taps[:, 0:5], raw[:, MP_VEC:MP_VEC + 5], ACT.Copy, scale=0.5)
                    act.activation(prev[:, 0:3], raw[:, MP_CS:MP_CS + 3], ACT.Copy)
                    act.activation(s_init[:], raw[:, MP_ST:MP_ST + P], ACT.Copy).then_inc(ph["vec"], 1)

                def convolve(g, t, s):
                    c = s % 2
                    done(act, "ip", g)
                    done(act, "xs", g - 1)
                    done(act, "vec", t)
                    act.wait_ge(ph["xb"], g + CR["xb"])
                    before = xbuf[:, 1 - c, TS:TS + 3] if s else prev[:, 0:3]
                    act.activation(xbuf[:, c, 0:3], before, ACT.Copy)
                    act.activation(xbuf[:, c, 3:3 + TS], bank[:, 1, :], ACT.Copy).then_inc(ph["xb"], 1)
                    act.activation(cv[:], bank[:, 1, :], ACT.Identity, bias=taps[:, 4:5], scale=taps[:, 3:4])\
                        .then_inc(ph["c0"], 1)
                    done(act, "zs", g - 1)
                    act.activation(tz[:], bank[:, 0, :], ACT.Tanh, scale=0.5).then_inc(ph["tz"], 1)

                def decays(g, s):
                    done(act, "arg", g)
                    act.activation(mt[:], mt[:], ACT.Exp).then_inc(ph["ex"], 1)
                    done(act, "state", g - 2, NJ)
                    act.activation(dec[:, s % 2], a_wide[:, :, s * TS + P - 1:(s + 1) * TS:P], ACT.Exp).then_inc(ph["dec"], 1)

                def tanh(g):
                    done(act, "tap", g, NR - 1)
                    act.activation(th[:], cv[:], ACT.Tanh).then_inc(ph["th"], 1)

                def finish(g):
                    done(act, "y", g)
                    done(act, "y2", g - 1)
                    act.activation(ys[:], y[:], ACT.Square).then_inc(ph["ys"], 1)
                    done(act, "yz", g)
                    done(act, "out", g - 1)
                    act.activation(yz_hi[:], yz[:], ACT.Copy).then_inc(ph["hi"], 1)

                def emit(t, first, last):
                    for s in range(NS):
                        g = t * NS + s
                        done(act, "xt", g)
                        done(act, "intra", g - 1)
                        act.activation(x_tok[:].rearrange("p j c -> p (j c)"), bank[:, 2, :], ACT.Copy)\
                            .then_inc(ph["x_tok"], 1)
                        if not (first and s == 0):
                            finish(g - 1)
                        if s == 0:
                            done(act, "t2", g - 1)
                            act.activation(skip[:], raw[:, MP_VEC + 5:MP_VEC + 6], ACT.Copy).then_inc(ph["skip"], 1)
                        if s == 1:
                            done(act, "wo_s", t)
                            done(act, "out", t * NS - 1)
                            act.activation(wo_hi[:], wo_s[:], ACT.Copy).then_inc(ph["wo_hi"], 1)
                        act.wait_ge(ph[f"feat{s}"], t * 32 + 32)
                        done(act, "t1", g - 1)
                        act.activation(ea[:], a_feat[:, step(s)], ACT.Exp).then_inc(ph["ea"], 1)
                        if last and s == NS - 1:
                            break
                        n = (s + 1) % NS
                        convolve(g + 1, t + (s == NS - 1), n)
                        if s == NS - 2 and not last:
                            take_weights(t + 1)
                        tanh(g + 1)
                        decays(g + 1, n)
                        if s == NS - 2 and not last:
                            take_vectors(t + 1, False)

                credit(act, "scalar")
                take_weights(0)
                take_vectors(0, True)
                convolve(0, 0, 0)
                decays(0, 0)
                tanh(0)
                tiles(act, emit)
                finish(NCT * NS - 1)
                done(act, "yms_eps", 0)
                act.activation(y2[:], y2[:], ACT.Sqrt).then_inc(ph["ysd"], 1)

            @block.gpsimd
            def _(pl):
                def decayed(g, s):
                    done(pl, "ex", g)
                    done(pl, "intra", g - 1)
                    pl.tensor_tensor(mm[:], mt[:], cb[:, s * NJ:(s + 1) * NJ, :].rearrange("p j t -> p (j t)")
                                     .unsqueeze(1).broadcast_to([P, 2, TS]), ALU.mult).then_inc(ph["mm"], 1)

                def outputs(g, s):
                    done(pl, "t1", g)
                    done(pl, "t2", g)
                    done(pl, "ys", g - 1)
                    pl.tensor_tensor(y[:], t1[:], t2[:], ALU.add).then_inc(ph["y"], 1)
                    done(pl, "y", g)
                    done(pl, "zs", g)
                    done(pl, "lo", g - 1)
                    pl.tensor_tensor(yz[:], y[:], zs[:, s % 2], ALU.mult).then_inc(ph["yz"], 1)

                def squares(g, s):
                    done(pl, "ys", g)
                    done(pl, "y2", g - 1)
                    pl.tensor_tensor(y2[:, step(s)], y2[:, step(s)], ys[:], ALU.add).then_inc(ph["y2"], 1)

                def emit(t, first, last):
                    for s in range(NS):
                        g = t * NS + s
                        decayed(g, s)
                        if not (first and s == 0):
                            outputs(g - 1, (s - 1) % NS)
                            squares(g - 1, (s - 1) % NS)
                pl.memset(y2[:], 0.0).then_inc(ph["y2"], 1)
                credit(pl, "gpsimd")
                tiles(pl, emit)
                outputs(NCT * NS - 1, NS - 1)
                squares(NCT * NS - 1, NS - 1)

            @block.vector
            def _(dve):
                def low_in(t):
                    done(dve, "wi_hi", t)
                    dve.tensor_tensor(wi_lo[:], raw[:, 0:MP_IN], wi_hi[:].bitcast(F32), ALU.subtract).then_inc(ph["wi_lo"], 1)

                def front(g, s):
                    c = s % 2
                    done(dve, "tz", g)
                    done(dve, "yz", g - 2)
                    dve.scalar_tensor_tensor(zs[:, c], tz[:], 1.0, bank[:, 0, :], ALU.add, ALU.mult).then_inc(ph["zs"], 1)
                    done(dve, "xb", g)
                    done(dve, "c0", g)
                    for k in range(NR - 1):
                        if k:
                            dve.wait_ge(ph["tap"], g * (NR - 1) + k)
                        dve.scalar_tensor_tensor(cv[:], xbuf[:, c, k:k + TS], taps[:, k:k + 1], cv[:], ALU.mult, ALU.add)\
                            .then_inc(ph["tap"], 1)

                def differences(g, t, s):
                    if s == 0:
                        done(dve, "arg", g - 1)
                        dve.tensor_copy(a_here[:], a_tok[:, :, bass.ds(t * 2, 2)]).then_inc(ph["a_here"], 1)
                        done(dve, "a_here", t)
                    dve.wait_ge(ph[f"wide{s}"], (t + 1) * 16)
                    done(dve, "mm", g - 1)
                    for h in range(2):
                        for j in range(NJ):
                            a = s * TS + j * P
                            i = dve.tensor_scalar(mt[:, h, j * P:(j + 1) * P], a_wide[:, h, a:a + P],
                                                  a_here[:, s * NJ + j, h:h + 1], 0.0, ALU.subtract, ALU.min)
                    i.then_inc(ph["arg"], 1)

                def silu(g, s):
                    done(dve, "th", g)
                    done(dve, "t2", g - 2)
                    dve.scalar_tensor_tensor(xs[:, s % 2], th[:], 1.0, cv[:], ALU.add, ALU.mult).then_inc(ph["xs"], 1)

                def add(g, s):
                    done(dve, "out", g)
                    done(dve, "added", g - 1)
                    dve.tensor_tensor(proj[:, :, step(s)], bank[:, 6:8, :], proj[:, :, step(s)], ALU.add)\
                        .then_inc(ph["added"], 1)

                def low_out(g):
                    done(dve, "hi", g)
                    dve.tensor_tensor(yz_lo[:], yz[:], yz_hi[:].bitcast(F32), ALU.subtract).then_inc(ph["lo"], 1)

                def scan(g, t, s):
                    done(dve, "u", g)
                    done(dve, "dec", g)
                    done(dve, "inter", g - 1)
                    for j in range(NJ):
                        dve.wait_ge(ph["state"], g * NJ + j + CR["state"])
                        if j:
                            before = state[:, s % 2, j - 1]
                        else:
                            before = state[:, 1 - s % 2, NJ - 1] if s else s_init[:]
                        for h in range(2):
                            hs = slice(h * PH, (h + 1) * PH)
                            i = dve.scalar_tensor_tensor(state[:, s % 2, j, hs], before[:, hs], dec[:, s % 2, h, j:j + 1],
                                                         bank[:, 5, j * P + h * PH:j * P + (h + 1) * PH], ALU.mult, ALU.add)
                        i.then_inc(ph["state"], 1)

                def emit(t, first, last):
                    for s in range(NS):
                        g = t * NS + s
                        if s == 0:
                            done(dve, "xd", g - 1)
                            dve.tensor_copy(w_here[:], w_tok[:, :, bass.ds(t * 2, 2)]).then_inc(ph["w_here"], 1)
                            done(dve, "w_here", t)
                        done(dve, "x_tok", g)
                        done(dve, "u", g - 1)
                        dve.tensor_tensor(xd[:].rearrange("p j (h c) -> p j h c", h=2),
                                          bank[:, 2, :].rearrange("p (j h c) -> p j h c", j=NJ, h=2),
                                          w_here[:, s * NJ:(s + 1) * NJ, :].unsqueeze(3)
                                          .broadcast_to([P, NJ, 2, PH]), ALU.mult).then_inc(ph["xd"], 1)
                        more = not (last and s == NS - 1)
                        if more:
                            differences(g + 1, t + (s == NS - 1), (s + 1) % NS)
                        if not (first and s == 0):
                            low_out(g - 1)
                        if s == 0:
                            dve.wait_ge(ph["raw"], t * 16 + 16)
                            dve.tensor_scalar(wo_s[:], raw[:, MP_IN:MP_VEC], raw[:, MP_VEC + 6:MP_VEC + 7], 0.5,
                                              ALU.mult, ALU.mult).then_inc(ph["wo_s"], 1)
                        if s == 1:
                            done(dve, "wo_hi", t)
                            dve.tensor_tensor(wo_lo[:], wo_s[:], wo_hi[:].bitcast(F32), ALU.subtract).then_inc(ph["wo_lo"], 1)
                        scan(g, t, s)
                        if more:
                            front(g + 1, (s + 1) % NS)
                        if s == NS - 2 and not last:
                            low_in(t + 1)
                        done(dve, "intra", g)
                        done(dve, "skip", t)
                        done(dve, "y", g - 1)
                        dve.scalar_tensor_tensor(t2[:], xs[:, s % 2], skip[:], bank[:, 3, :], ALU.mult, ALU.add)\
                            .then_inc(ph["t2"], 1)
                        done(dve, "inter", g)
                        done(dve, "ea", g)
                        dve.tensor_tensor(t1[:], bank[:, 4, :], ea[:], ALU.mult).then_inc(ph["t1"], 1)
                        if more:
                            silu(g + 1, (s + 1) % NS)
                        if not (first and s == 0):
                            add(g - 1, (s - 1) % NS)

                dve.memset(proj[:], 0.0).then_inc(ph["added"], 1)
                credit(dve, "vector")
                low_in(0)
                differences(0, 0, 0)
                front(0, 0)
                silu(0, 0)
                tiles(dve, emit)
                low_out(NCT * NS - 1)
                add(NCT * NS - 1, NS - 1)
                done(dve, "yms", 0)
                dve.tensor_scalar_add(y2[:], bank[:, 0:NS, :].rearrange("p s t -> p (s t)"), 1e-5).then_inc(ph["yms_eps"], 1)
                done(dve, "ysd", 0)
                dve.reciprocal(a_feat[:], y2[:]).then_inc(ph["yr"], 1)
                done(dve, "yr", 0)
                done(dve, "added", NCT * NS - 1)
                dve.tensor_tensor(proj[:], proj[:], a_feat[:].unsqueeze(1).broadcast_to([P, KD, T]), ALU.mult)\
                    .then_inc(ph["yr"], 1)
                done(dve, "yr", 1)
                dve.tensor_tensor(acc[:], acc[:], proj[:], ALU.add)
        ph.clear()


def kernel(**inputs):
    import numpy as np
    import concourse.bacc as bacc
    from concourse.bass_utils import run_bass_kernel_spmd as run

    w = {n: np.asarray(a) for n, a in inputs.items()}

    def feat(a):
        return a.reshape(KD, P, -1).transpose(1, 0, 2)

    x = w["L0_attn_x"]
    arrays = {"xT": x.transpose(0, 2, 1).reshape(B, KD, P, T).transpose(0, 2, 1, 3)}

    tab = np.zeros((P, TABLE_W), np.float32)

    def put(name, a):
        a = np.asarray(a, np.float32)
        a0, _ = _cols[name]
        a = a.reshape(a.shape[0], -1)
        tab[0:a.shape[0], a0:a0 + a.shape[1]] = a

    p, f = np.arange(P)[:, None], np.arange(TS)[None, :]
    put("ident", np.eye(P))
    put("mean", np.full((P, P), 1.0 / D))
    put("mean32", (p // HV == f[:, :P] // HV) / float(HV))
    put("mean_di", np.full((P, P), 1.0 / DI))
    put("scan64", np.broadcast_to(f % CH != 0, (P, TS)))
    put("scan128", np.broadcast_to(f % P != 0, (P, TS)))
    put("causal64", p % CH <= f[:, :CH])
    put("causal128", p <= f[:, :P])
    put("headmask", p // HK == f[:, :H0])
    put("bdmask", p // HK == f[:, :D] // HV)
    put("iota", np.broadcast_to(f[:, :NE], (P, NE)))
    put("bias0", np.broadcast_to(w["L0_ffn_extra_bias"], (P, E0)))
    put("scale0", np.broadcast_to(w["L0_ffn_extra_scale"], (P, E0)))
    put("norm1", feat(w["L0_attn_norm1_w"]))
    put("ffn_norm", feat(w["L0_attn_ffn_norm_w"]))
    put("norm_m", feat(w["L1_attn_norm_w"]))
    put("gk_b", w["L0_attn_gk_b"][:, None])
    put("gnorm", np.tile(w["L0_attn_gnorm_w"], P // HV)[:, None])
    put("dt_bias", w["L1_attn_dt_bias"][:, None])
    put("A_log", w["L1_attn_A_log"][:, None])
    put("router0", feat(np.concatenate([w["L0_ffn_cls_w"].T, w["L0_ffn_gate_w"].T], 1)))
    put("router1", feat(w["L1_ffn_router_w"]))
    put("gk1", feat(w["L0_attn_gk_w1"]))
    put("gk2", w["L0_attn_gk_w2"])
    win = w["L1_attn_in_proj_w"]
    put("wdt", feat(win[2 * DI + 2 * NST:].T))
    arrays["table"] = tab

    arrays["gla_w"] = feat(np.concatenate([w["L0_attn_wq"], w["L0_attn_wk"], w["L0_attn_wg"], w["L0_attn_wv"]], 1))
    arrays["gla_wo"] = feat(w["L0_attn_wo"])
    arrays["wbc"] = feat(win[2 * DI:2 * DI + 2 * NST].T)

    def hidden_tiles(gate, up, down):
        n = gate.shape[0] // P
        gu = np.stack([gate, up]).reshape(2, n, P, KD, P).transpose(1, 4, 3, 0, 2).reshape(n, P, -1)
        return np.concatenate([gu, down.reshape(n, P, D)], 2)

    def by_expert(a):
        return a.reshape(NE, -1, 8, D).transpose(1, 0, 2, 3).reshape(-1, D)

    def padded(a):
        n = -a.shape[0] % (2 * P)
        return np.concatenate([a, np.zeros((n, D), a.dtype)])

    arrays["ffn0"] = hidden_tiles(padded(w["L0_attn_w_gate"].T), padded(w["L0_attn_w_up"].T), padded(w["L0_attn_w_down"]))
    parts = []
    for routed, shared, down in (("wg", "sg", False), ("wu", "su", False), ("wd", "sd", True)):
        r, s = w["L0_ffn_" + routed], w["L0_ffn_" + shared]
        if down:
            r, s = r.transpose(0, 2, 1), s.T
        parts.append(by_expert(np.concatenate([r, s.reshape(NE - E0, -1, D)])))
    arrays["moe0"] = hidden_tiles(*parts)
    arrays["moe1"] = hidden_tiles(by_expert(w["L1_ffn_gate_w"].transpose(0, 2, 1)),
                                  by_expert(w["L1_ffn_up_w"].transpose(0, 2, 1)), by_expert(w["L1_ffn_down_w"]))

    zx = win[:2 * DI].reshape(2, NCT, P, KD, P).transpose(1, 4, 3, 0, 2).reshape(NCT, P, -1)
    vec = np.zeros((NCT, P, 8), np.float32)
    vec[:, :, 0:4] = w["L1_attn_conv_w"].reshape(NCT, P, NR)
    vec[:, :, 4] = w["L1_attn_conv_b"].reshape(NCT, P)
    vec[:, :, 5] = np.repeat(w["L1_attn_D_param"], PH).reshape(NCT, P)
    vec[:, :, 6] = w["L1_attn_inner_norm_w"].reshape(NCT, P)
    cs = np.zeros((NCT, P, 4), np.float32)
    cs[:, :, 0:3] = w["L1_attn_conv_state"].reshape(NCT, P, NR - 1)
    init = w["L1_attn_ssm_state"].reshape(NCT, 2, NST, PH).transpose(0, 2, 1, 3).reshape(NCT, P, P)
    arrays["mamba"] = np.concatenate([zx, w["L1_attn_out_proj_w"].T.reshape(NCT, P, D), vec, cs, init], 2)

    nc = bacc.Bacc("TRN2", target_bir_lowering=False, num_devices=1)
    arrays = {n: np.ascontiguousarray(a) for n, a in arrays.items()}
    aps = {n: nc.dram_tensor(n + "_dram", a.shape, F32, kind="ExternalInput").ap() for n, a in arrays.items()}
    a_dram = nc.dram_tensor("a_scratch", (HM, T), F32, kind="Internal").ap()
    out = nc.dram_tensor("out_dram", (B, P, KD, T), F32, kind="ExternalOutput").ap()
    program(nc, a_dram=a_dram, outT=out, **aps)
    r = run(nc, [{n + "_dram": a for n, a in arrays.items()}], core_ids=[0])
    y = r.results[0]["out_dram"]
    return np.ascontiguousarray(y.transpose(0, 2, 1, 3).reshape(B, D, T).transpose(0, 2, 1))
```

```python
from contextlib import ExitStack

import concourse.bass as bass
from concourse import mybir

F32 = mybir.dt.float32
F32R = mybir.dt.float32r
U32 = mybir.dt.uint32
ACT = mybir.ActivationFunctionType
ALU = mybir.AluOpType
AX = mybir.AxisListType

P = 128
B, T, D = 2, 2048, 256
KD = D // P
TS = 512
NS = T // TS
NJ = TS // P

H0, HK, HV, CH = 8, 16, 32, 64
NC0 = TS // CH
LR = 16
GNORM = 16.0
E0, NE = 14, 16
HM, PH, NST = 48, 64, 128
DI = HM * PH
NCT = DI // P
NR = 4
MLP_W = 2 * KD * P + D
MP_IN, MP_OUT = 2 * KD * P, D
MP_VEC = MP_IN + MP_OUT
MP_CS = MP_VEC + 8
MP_ST = MP_CS + 4
MP_W = MP_ST + P

_cols = {}
_at = 0
for _n, _w in (("ident", P), ("mean", P), ("mean32", P), ("mean_di", P), ("scan64", TS), ("scan128", TS),
               ("causal64", CH), ("causal128", P), ("headmask", H0), ("bdmask", D), ("iota", NE),
               ("bias0", E0), ("scale0", E0), ("norm1", KD), ("ffn_norm", KD), ("norm_m", KD),
               ("eps6", 1), ("eps5", 1), ("gk_b", 1), ("gnorm", 1), ("dt_bias", 1), ("A_log", 1),
               ("router0", KD * 2 * E0), ("router1", KD * NE), ("gk1", KD * LR), ("gk2", P), ("wdt", KD * HM)):
    _cols[_n] = (_at, _at + _w)
    _at += _w
TABLE_W = _at


def mm3(pe, out, w, x, first=True, last=True):
    (wh, wl), (xh, xl) = w, x
    pe.matmul(out, wh, xh, start=first, stop=False)
    pe.matmul(out, wh, xl, start=False, stop=False)
    return pe.matmul(out, wl, xh, start=False, stop=last)


class Phase:

    def __init__(self, nc, pool):
        self.nc, self.pool, self.names = nc, pool, {}

    def __getitem__(self, name):
        if name not in self.names:
            self.names[name] = self.pool[len(self.names)]
        return self.names[name]

    def clear(self):
        first = self.pool[0].num
        self.nc.sync.sem_clear(range(first, first + len(self.names)))
        self.nc.all_engine_barrier(sem_only=True)


def need(eng, sig, **counts):
    for name, n in counts.items():
        eng.wait_ge(sig[name], n)


def rsqrt(act, ph, out, x, eps, name):
    act.activation(out, x, ACT.Ln, bias=eps).then_inc(ph[name + "_ln"], 1)
    need(act, ph, **{name + "_ln": 1})
    act.activation(out, out, ACT.Exp, scale=-0.5).then_inc(ph[name], 1)


def program(nc, xT, table, gla_w, gla_wo, wbc, moe0, ffn0, moe1, mamba, a_dram, outT):
    ctx = ExitStack()
    with ctx:
        pool = [ctx.enter_context(nc.semaphore(f"sig{i}")) for i in range(100)]
        assert [s.num for s in pool] == list(range(pool[0].num, pool[0].num + len(pool)))

        def sb(name, shape, dt=F32, where=ctx):
            return where.enter_context(nc.sbuf_tensor(name, shape, dt))

        bank = ctx.enter_context(nc.psum_tensor("bank", [P, 8, TS], F32))

        tab = sb("tab", [P, TABLE_W])
        acc = sb("acc", [P, KD, T])
        f_hi = sb("f_hi", [P, KD, T], F32R)
        f_lo = sb("f_lo", [P, KD, T], F32R)

        def col(name):
            a, b = _cols[name]
            return tab[:, a:b]

        def colk(name, k=KD):
            return col(name).rearrange("p (k c) -> p k c", k=k)

        ident = col("ident")

        with nc.Block(no_gpsimd_drain=True) as block:
            ph = Phase(nc, pool)

            @block.sync
            def _(sp):
                sp.dma_start(tab[:], table).then_inc(ph["table"], 16)
                sp.wait_ge(ph["table"], 16)
        ph.clear()

        with nc.Fori(0, B) as b:
            with ExitStack() as own:
                e_hi = sb("e_hi", [P, KD, T], F32R, own)
                e_lo = sb("e_lo", [P, KD, T], F32R, own)
                cw = sb("cw", [P, T], F32, own)
                attention(nc, pool, bank, b, xT, gla_w, gla_wo, acc, e_hi, e_lo, f_hi, f_lo, cw, col, colk)
                mlp(nc, pool, bank, "ffn", ffn0, f_hi, f_lo, None, acc)
                mlp(nc, pool, bank, "moe0", moe0, e_hi, e_lo, cw, acc)
            with ExitStack() as layer1:
                st = {n: sb(n, shape, F32, layer1) for n, shape in (
                    ("b_tok", [P, T // P, NST]),
                    ("c_feat", [P, T]),
                    ("cb", [P, T // P, P]),
                    ("a_tok", [P, T // P, HM]),
                    ("w_tok", [P, T // P, HM]))}
                with ExitStack() as own:
                    e_hi = sb("e1_hi", [P, KD, T], F32R, own)
                    e_lo = sb("e1_lo", [P, KD, T], F32R, own)
                    cw = sb("cw1", [P, T], F32, own)
                    ssm_prepare(nc, pool, bank, wbc, a_dram, acc, e_hi, e_lo, f_hi, f_lo, cw, st, col, colk)
                    mlp(nc, pool, bank, "moe1", moe1, e_hi, e_lo, cw, acc)
                ssm(nc, pool, bank, mamba, a_dram, acc, f_hi, f_lo, st, col)
            with nc.Block(no_gpsimd_drain=True) as block:
                ph = Phase(nc, pool)

                @block.sync
                def _(sp):
                    sp.dma_start(outT[bass.ds(b, 1)].rearrange("o p k t -> (o p) k t"), acc[:]).then_inc(ph["out"], 16)
                    sp.wait_ge(ph["out"], 16)
            ph.clear()


def attention(nc, pool, bank, b, xT, gla_w, gla_wo, acc, e_hi, e_lo, f_hi, f_lo, cw, col, colk):
    with ExitStack() as own:
        def sb(name, shape, dt=F32):
            return own.enter_context(nc.sbuf_tensor(name, shape, dt))

        w_hi, w_lo = sb("gw_hi", [P, KD, 768], F32R), sb("gw_lo", [P, KD, 768], F32R)
        wo_hi, wo_lo = sb("gwo_hi", [P, KD, D], F32R), sb("gwo_lo", [P, KD, D], F32R)
        state = sb("state", [P, 2, D])
        x = sb("x", [P, KD, TS])

        def load_x(sp, t0):
            sp.dma_start(x[:], xT[bass.ds(b, 1), :, :, bass.ds(t0, TS)].rearrange("o p k t -> (o p) k t"))\
                .then_inc(ph["x"], 16)

        ph = Phase(nc, pool)
        with (nc.sbuf_tensor("gw_raw", [P, KD, 768], F32) as w_raw, nc.sbuf_tensor("gwo_raw", [P, KD, D], F32) as wo_raw,
              nc.Block(no_gpsimd_drain=True) as block):
            @block.sync
            def _(sp):
                sp.dma_start(w_raw[:], gla_w).then_inc(ph["raw"], 16)
                sp.dma_start(wo_raw[:], gla_wo).then_inc(ph["raw"], 16)
                load_x(sp, 0)
                sp.wait_ge(ph["raw"], 32)
                sp.wait_ge(ph["x"], 16)

            @block.vector
            def _(dve):
                dve.memset(state[:], 0.0)
                dve.wait_ge(ph["raw"], 32)
                dve.tensor_copy(w_hi[:], w_raw[:]).then_inc(ph["hi"], 1)
                dve.tensor_copy(wo_hi[:], wo_raw[:]).then_inc(ph["hi"], 1)
                dve.wait_ge(ph["hi"], 2)
                dve.tensor_tensor(w_lo[:], w_raw[:], w_hi[:].bitcast(F32), ALU.subtract)
                dve.tensor_tensor(wo_lo[:], wo_raw[:], wo_hi[:].bitcast(F32), ALU.subtract)
        ph.clear()

        xc = sb("xc", [P, KD, TS])
        sq = sb("sq", [P, KD, TS])
        r = sb("r", [P, 6, TS])
        xn = sb("xn", [P, KD, TS])
        h = sb("h", [P, KD, TS])
        h_hi, h_lo = sb("h_hi", [P, KD, TS], F32R), sb("h_lo", [P, KD, TS], F32R)
        rt = router_tiles(sb, "rt0_")
        lowrank = sb("lowrank", [LR, TS])
        v = sb("v", [P, NJ, D])
        sgate = sb("sgate", [P, KD, TS])
        g = sb("g", [P, 8, TS])
        qe, ke, kl = sb("qe", [P, TS]), sb("ke", [P, TS]), sb("kl", [P, TS])
        klt = sb("klt", [P, NJ, P])
        qb = sb("qb", [P, 2, H0, CH])
        am = sb("am", [P, 2, H0, CH])
        um = sb("um", [P, 2, D])
        on = sb("on", [P, KD, TS])
        og_hi, og_lo = h_hi, h_lo

        def both(a):
            return a.unsqueeze(1).broadcast_to([P, KD, TS])

        def by_chunk(a):
            return a.rearrange("p (j u c) -> p j u c", j=NJ, u=2)

        def heads_out(gr):
            return bank[:, 0:2, gr * NJ * CH:(gr + 1) * NJ * CH].rearrange("p u (j c) -> p j u c", j=NJ)

        def run(s, last):
            nonlocal ph
            ph = Phase(nc, pool)
            t0 = s * TS
            ts = bass.ds(t0, TS)
            gk, mn, e1, l1, gs, cum, eb, enb = (g[:, i, :] for i in range(8))
            with nc.Block(no_gpsimd_drain=True) as block:

                @block.sync
                def _(sp):
                    if not last:
                        need(sp, ph, acc=1)
                        load_x(sp, t0 + TS)
                        sp.wait_ge(ph["x"], 16)

                @block.tensor
                def _(pe):
                    for k in range(KD):
                        i = pe.matmul(bank[:, 0, :], col("mean"), x[:, k, :], start=k == 0, stop=k == KD - 1)
                    i.then_inc(ph["mean"], 1)
                    need(pe, ph, sq=1)
                    for k in range(KD):
                        i = pe.matmul(bank[:, 1, :], col("mean"), sq[:, k, :], start=k == 0, stop=k == KD - 1)
                    i.then_inc(ph["var"], 1)
                    need(pe, ph, xn=1)
                    router_logits(pe, ph, bank, xn, colk("router0"), 2 * E0)
                    need(pe, ph, h_hi=1, h_lo=1)
                    for n, dst in ((0, 4), (1, 5)):
                        for k in range(KD):
                            c = slice(n * P, n * P + P)
                            i = mm3(pe, bank[:, dst, :], (w_hi[:, k, c], w_lo[:, k, c]),
                                    (h_hi[:, k, :], h_lo[:, k, :]), k == 0, k == KD - 1)
                    i.then_inc(ph["qk"], 1)
                    for k in range(KD):
                        i = pe.matmul(bank[0:LR, 6, :], colk("gk1")[:, k, :], h[:, k, :], start=k == 0, stop=k == KD - 1)
                    i.then_inc(ph["rank_ps"], 1)
                    need(pe, ph, r1=1)
                    for j in range(NJ):
                        o = bank[:, j // 2, (j % 2) * D:(j % 2) * D + D]
                        for k in range(KD):
                            js = slice(j * P, j * P + P)
                            i = mm3(pe, o, (h_hi[:, k, js], h_lo[:, k, js]), (w_hi[:, k, 512:768], w_lo[:, k, 512:768]),
                                    k == 0, k == KD - 1)
                    i.then_inc(ph["v_ps"], 1)
                    need(pe, ph, rank=1)
                    pe.matmul(bank[:, 7, :], col("gk2")[0:LR, :], lowrank[:], start=True, stop=True).then_inc(ph["gk_ps"], 1)
                    router_transpose(pe, ph, bank, rt, col("ident"))
                    need(pe, ph, cw=1)
                    for n in range(KD):
                        for k in range(KD):
                            c = slice(256 + n * P, 256 + n * P + P)
                            i = mm3(pe, bank[:, 2 + n, :], (w_hi[:, k, c], w_lo[:, k, c]),
                                    (h_hi[:, k, :], h_lo[:, k, :]), k == 0, k == KD - 1)
                    i.then_inc(ph["gate_ps"], 1)
                    need(pe, ph, kl=1)
                    for j in range(NJ):
                        i = pe.transpose(bank[:, 6, j * P:(j + 1) * P], kl[:, j * P:(j + 1) * P], col("ident"))
                    i.then_inc(ph["klt_ps"], 1)
                    need(pe, ph, v=1, klt=1, ke=1)
                    for j in range(NJ):
                        a = bank[:, 4 + j % 2, :]
                        if j >= 2:
                            need(pe, ph, am=j - 1)
                        for u in range(2):
                            c = 2 * j + u
                            need(pe, ph, qb=c + 1)
                            i = pe.matmul(a[u * CH:(u + 1) * CH, :], ke[:, c * CH:(c + 1) * CH],
                                          qb[:, u].rearrange("p h c -> p (h c)"), start=True, stop=True)
                            i.then_inc(ph["a_ps"], 1)
                        for u in range(2):
                            c = 2 * j + u
                            rows = slice(u * CH, (u + 1) * CH)
                            if c >= 2:
                                need(pe, ph, um=c - 1)
                            pe.matmul(bank[:, 6 + u, 0:D], klt[rows, j, :], v[rows, j, :], start=True, stop=True)\
                                .then_inc(ph["u_ps"], 1)
                        need(pe, ph, am=j + 1)
                        for u in range(2):
                            c = 2 * j + u
                            rows = slice(u * CH, (u + 1) * CH)
                            if c:
                                need(pe, ph, state=c)
                            for gr in range(2):
                                o = bank[:, u, (gr * NJ + j) * CH:(gr * NJ + j + 1) * CH]
                                pe.matmul(o, state[:, c % 2, gr * P:(gr + 1) * P], qe[:, c * CH:(c + 1) * CH],
                                          start=True, stop=False)
                                for q in range(4):
                                    hh = 4 * gr + q
                                    i = pe.matmul(o[q * HV:(q + 1) * HV, :], v[rows, j, hh * HV:(hh + 1) * HV],
                                                  am[rows, j % 2, hh, :], start=False, stop=True,
                                                  tile_position=(u * CH, q * HV))
                            i.then_inc(ph["o_ps"], 1)
                    need(pe, ph, sqo=2)
                    for gr in range(2):
                        i = pe.matmul(bank[:, 4 + gr, :], col("mean32"), sq[:, gr, :], start=True, stop=True)
                    i.then_inc(ph["hms"], 1)
                    need(pe, ph, og_hi=1, og_lo=1)
                    for n in range(KD):
                        for k in range(KD):
                            c = slice(n * P, n * P + P)
                            i = mm3(pe, bank[:, 2 + n, :], (wo_hi[:, k, c], wo_lo[:, k, c]),
                                    (og_hi[:, k, :], og_lo[:, k, :]), k == 0, k == KD - 1)
                    i.then_inc(ph["gla_ps"], 1)
                    need(pe, ph, sqy=1)
                    for k in range(KD):
                        i = pe.matmul(bank[:, 6, :], col("mean"), sq[:, k, :], start=k == 0, stop=k == KD - 1)
                    i.then_inc(ph["yms"], 1)

                @block.scalar
                def _(act):
                    need(act, ph, xc=1)
                    act.activation(sq[:], xc[:], ACT.Square).then_inc(ph["sq"], 1)
                    need(act, ph, var=1)
                    rsqrt(act, ph, r[:, 5, :], bank[:, 1, :], col("eps5"), "rstd")
                    need(act, ph, vrr=1)
                    rsqrt(act, ph, r[:, 2, :], r[:, 3, :], col("eps6"), "r1")
                    need(act, ph, xn=1)
                    act.activation(e_hi[:, :, ts], xn[:], ACT.Copy).then_inc(ph["xn_hi"], 1)
                    need(act, ph, h=KD)
                    act.activation(h_hi[:], h[:], ACT.Copy).then_inc(ph["h_hi"], 1)
                    need(act, ph, rank_ps=1)
                    act.activation(lowrank[:], bank[0:LR, 6, :], ACT.Copy).then_inc(ph["rank"], 1)
                    need(act, ph, v_ps=1)
                    act.activation(v[:].rearrange("p j d -> p (j d)"),
                                   bank[:, 0:2, :].rearrange("p j d -> p (j d)"), ACT.Copy).then_inc(ph["v"], 1)
                    need(act, ph, logits=1)
                    act.activation(rt["gate"][:], bank[:, 2, 0:NJ * 2 * E0]
                                   .rearrange("p (j e) -> p j e", j=NJ)[:, :, E0:2 * E0], ACT.Silu).then_inc(ph["rgate"], 1)
                    need(act, ph, shifted=1)
                    act.activation(rt["ex"][:, :, 0:E0], rt["sh"][:, :, 0:E0], ACT.Exp).then_inc(ph["rexp"], 1)
                    need(act, ph, gk_ps=1)
                    act.activation(gk, bank[:, 7, :], ACT.Abs, bias=col("gk_b")).then_inc(ph["absz"], 1)
                    need(act, ph, absz=1)
                    act.activation(e1, gk, ACT.Exp, scale=-1.0).then_inc(ph["e1"], 1)
                    need(act, ph, e1=1)
                    act.activation(l1, e1, ACT.Ln, bias=1.0).then_inc(ph["l1"], 1)
                    need(act, ph, cum=1)
                    act.activation(eb, cum, ACT.Exp, scale=1.0 / GNORM).then_inc(ph["eb"], 1)
                    act.activation(enb, cum, ACT.Exp, scale=-1.0 / GNORM).then_inc(ph["enb"], 1)
                    need(act, ph, rest=1)
                    act.activation(e1, mn, ACT.Exp, scale=1.0 / GNORM).then_inc(ph["el"], 1)
                    need(act, ph, cwt_ps=1)
                    act.activation(cw[:, ts], bank[:, 3, :], ACT.Copy).then_inc(ph["cw"], 1)
                    need(act, ph, gate_ps=1)
                    act.activation(sgate[:], bank[:, 2:4, :], ACT.Silu).then_inc(ph["sgate"], 1)
                    need(act, ph, klt_ps=1)
                    act.activation(klt[:].rearrange("p j k -> p (j k)"), bank[:, 6, :], ACT.Copy).then_inc(ph["klt"], 1)
                    need(act, ph, o_ps=NC0)
                    for gr in range(2):
                        act.activation(by_chunk(sq[:, gr, :]), heads_out(gr), ACT.Square).then_inc(ph["sqo"], 1)
                    need(act, ph, hms=1)
                    rsqrt(act, ph, on[:], bank[:, 4:6, :], col("eps6"), "hr")
                    need(act, ph, og=1)
                    act.activation(og_hi[:], on[:], ACT.Copy).then_inc(ph["og_hi"], 1)
                    need(act, ph, y=1)
                    act.activation(sq[:], xc[:], ACT.Square).then_inc(ph["sqy"], 1)
                    need(act, ph, yms=1)
                    rsqrt(act, ph, r[:, 4, :], bank[:, 6, :], col("eps6"), "r2")
                    need(act, ph, h2=KD)
                    act.activation(f_hi[:, :, ts], h[:], ACT.Copy).then_inc(ph["f_hi"], 1)

                @block.gpsimd
                def _(pool_):
                    need(pool_, ph, xn=1)
                    pool_.tensor_tensor(acc[:, :, ts], x[:], xn[:], ALU.add).then_inc(ph["acc"], 1)
                    need(pool_, ph, qe=1)
                    for c in range(NC0):
                        if c >= 2:
                            need(pool_, ph, a_ps=c - 1)
                        pool_.tensor_tensor(qb[:, c % 2], qe[:, c * CH:(c + 1) * CH].unsqueeze(1).broadcast_to([P, H0, CH]),
                                            col("headmask").unsqueeze(2).broadcast_to([P, H0, CH]), ALU.mult)\
                            .then_inc(ph["qb"], 1)

                @block.vector
                def _(dve):
                    need(dve, ph, mean=1)
                    dve.tensor_tensor(xc[:], x[:], both(bank[:, 0, :]), ALU.subtract).then_inc(ph["xc"], 1)
                    need(dve, ph, rstd=1)
                    dve.tensor_tensor(xn[:], xc[:], both(r[:, 5, :]), ALU.mult).then_inc(ph["xn"], 1)
                    dve.tensor_tensor(r[:, 2, :], bank[:, 1, :], r[:, 5, :], ALU.mult).then_inc(ph["vr"], 1)
                    need(dve, ph, vr=1)
                    dve.tensor_tensor(r[:, 3, :], r[:, 2, :], r[:, 5, :], ALU.mult).then_inc(ph["vrr"], 1)
                    need(dve, ph, r1=1, xn=1)
                    for k in range(KD):
                        dve.scalar_tensor_tensor(h[:, k, :], xn[:, k, :], col("norm1")[:, k:k + 1], r[:, 2, :],
                                                 ALU.mult, ALU.mult).then_inc(ph["h"], 1)
                    need(dve, ph, xn_hi=1)
                    dve.tensor_tensor(e_lo[:, :, ts], xn[:], e_hi[:, :, ts].bitcast(F32), ALU.subtract).then_inc(ph["e_lo"], 1)
                    need(dve, ph, h_hi=1)
                    dve.tensor_tensor(h_lo[:], h[:], h_hi[:].bitcast(F32), ALU.subtract).then_inc(ph["h_lo"], 1)
                    need(dve, ph, rgate=1)
                    lg = bank[:, 2, 0:NJ * 2 * E0].rearrange("p (j e) -> p j e", j=NJ)
                    dve.tensor_tensor(rt["lg"][:, :, 0:E0], lg[:, :, 0:E0], rt["gate"][:], ALU.mult).then_inc(ph["lg"], 1)
                    need(dve, ph, lg=1)
                    dve.scalar_tensor_tensor(rt["lg"][:, :, 0:E0], rt["lg"][:, :, 0:E0], -1.0, rt["lg"][:, :, 0:E0],
                                             ALU.mult, ALU.max).then_inc(ph["lg"], 1)
                    need(dve, ph, lg=2)
                    softmax(dve, ph, rt, E0)
                    dve.tensor_tensor(rt["bi"][:, :, 0:E0], rt["pr"][:, :, 0:E0],
                                      col("bias0").unsqueeze(1).broadcast_to([P, NJ, E0]), ALU.add).then_inc(ph["biased"], 1)
                    need(dve, ph, biased=1)
                    top2(dve, ph, rt, "bi", E0, col("iota"))
                    dve.tensor_tensor(rt["sh"][:, :, 0:E0], rt["pr"][:, :, 0:E0],
                                      col("scale0").unsqueeze(1).broadcast_to([P, NJ, E0]), ALU.mult).then_inc(ph["scaled"], 1)
                    need(dve, ph, scaled=1)
                    dve.scalar_tensor_tensor(rt["ex"][:, :, 0:E0], rt["sh"][:, :, 0:E0], 1.0, rt["pick"][:, :, 0:E0],
                                             ALU.add, ALU.mult).then_inc(ph["comb"], 1)
                    dve.memset(rt["ex"][:, :, E0:NE], 1.0).then_inc(ph["comb"], 1)
                    need(dve, ph, comb=2)
                    for j in range(NJ):
                        dve.tensor_copy(rt["rep"][:, j], rt["ex"][:, j].unsqueeze(2).broadcast_to([P, NE, 8]))\
                            .then_inc(ph["rep"], 1)
                    need(dve, ph, absz=1)
                    dve.tensor_scalar(mn, bank[:, 7, :], col("gk_b"), 0.0, ALU.add, ALU.min).then_inc(ph["minz"], 1)
                    need(dve, ph, l1=1, minz=1)
                    dve.tensor_tensor(gs, mn, l1, ALU.subtract).then_inc(ph["gs"], 1)
                    need(dve, ph, gs=1)
                    dve.tensor_tensor_scan(cum, col("scan64"), gs, 0.0, ALU.mult, ALU.add).then_inc(ph["cum"], 1)
                    need(dve, ph, cum=1, minz=1)
                    c3 = cum.rearrange("p (c t) -> p c t", c=NC0)
                    dve.tensor_tensor(mn.rearrange("p (c t) -> p c t", c=NC0),
                                      c3[:, :, CH - 1:CH].broadcast_to([P, NC0, CH]), c3, ALU.subtract).then_inc(ph["rest"], 1)
                    need(dve, ph, eb=1, qk=1)
                    dve.scalar_tensor_tensor(qe[:], bank[:, 4, :], HK ** -0.5, eb, ALU.mult, ALU.mult).then_inc(ph["qe"], 1)
                    need(dve, ph, enb=1)
                    dve.tensor_tensor(ke[:], bank[:, 5, :], enb, ALU.mult).then_inc(ph["ke"], 1)
                    need(dve, ph, el=1)
                    dve.tensor_tensor(kl[:], bank[:, 5, :], e1, ALU.mult).then_inc(ph["kl"], 1)
                    for j in range(NJ):
                        need(dve, ph, a_ps=2 * j + 2)
                        if j >= 2:
                            need(dve, ph, o_ps=2 * j - 2)
                        dve.tensor_tensor(am[:, j % 2], bank[:, 4 + j % 2, :].rearrange("p (h c) -> p h c", h=H0),
                                          col("causal64").unsqueeze(1).broadcast_to([P, H0, CH]), ALU.mult)\
                            .then_inc(ph["am"], 1)
                        for u in range(2):
                            c = 2 * j + u
                            need(dve, ph, u_ps=c + 1)
                            if c >= 2:
                                need(dve, ph, state=c - 1)
                            dve.tensor_tensor(um[:, u], bank[:, 6 + u, 0:D], col("bdmask"), ALU.mult).then_inc(ph["um"], 1)
                            need(dve, ph, um=c + 1)
                            if c:
                                need(dve, ph, o_ps=c, state=c)
                            dve.scalar_tensor_tensor(state[:, (c + 1) % 2], state[:, c % 2],
                                                     eb[:, (c + 1) * CH - 1:(c + 1) * CH], um[:, u],
                                                     ALU.mult, ALU.add).then_inc(ph["state"], 1)
                    need(dve, ph, hr=1)
                    for gr in range(2):
                        dve.tensor_tensor(by_chunk(xc[:, gr, :]), heads_out(gr), by_chunk(on[:, gr, :]), ALU.mult)\
                            .then_inc(ph["onorm"], 1)
                    need(dve, ph, onorm=2, sgate=1)
                    dve.scalar_tensor_tensor(on[:], xc[:], col("gnorm"), sgate[:], ALU.mult, ALU.mult).then_inc(ph["og"], 1)
                    need(dve, ph, og_hi=1)
                    dve.tensor_tensor(og_lo[:], on[:], og_hi[:].bitcast(F32), ALU.subtract).then_inc(ph["og_lo"], 1)
                    need(dve, ph, gla_ps=1, acc=1)
                    dve.tensor_tensor(acc[:, :, ts], bank[:, 2:4, :], acc[:, :, ts], ALU.add).then_inc(ph["acc"], 1)
                    dve.tensor_tensor(xc[:], bank[:, 2:4, :], xn[:], ALU.add).then_inc(ph["y"], 1)
                    need(dve, ph, r2=1, y=1, hr=1)
                    for k in range(KD):
                        dve.scalar_tensor_tensor(h[:, k, :], xc[:, k, :], col("ffn_norm")[:, k:k + 1], r[:, 4, :],
                                                 ALU.mult, ALU.mult).then_inc(ph["h2"], 1)
                    need(dve, ph, f_hi=1)
                    dve.tensor_tensor(f_lo[:, :, ts], h[:], f_hi[:, :, ts].bitcast(F32), ALU.subtract)
            ph.clear()

        with nc.Fori(0, NS - 1) as s:
            run(s, False)
        run(NS - 1, True)


def router_tiles(sb, tag):
    t = {n: sb(tag + n, [P, NJ, NE]) for n in ("lg", "sh", "ex", "pr", "bi", "pick", "one")}
    t["gate"] = sb(tag + "gate", [P, NJ, E0])
    t["m"] = sb(tag + "m", [P, NJ, 4])
    t["top"] = sb(tag + "top", [P, NJ, 8])
    t["idx"] = sb(tag + "idx", [P, NJ, 8], U32)
    t["idf"] = sb(tag + "idf", [P, NJ, 8])
    t["rep"] = sb(tag + "rep", [P, NJ, NE, 8])
    return t


def router_logits(pe, ph, bank, xn, w, n):
    for j in range(NJ):
        for k in range(KD):
            i = pe.matmul(bank[:, 2, j * n:(j + 1) * n], xn[:, k, j * P:(j + 1) * P], w[:, k, :],
                          start=k == 0, stop=k == KD - 1)
    i.then_inc(ph["logits"], 1)


def router_transpose(pe, ph, bank, rt, ident):
    need(pe, ph, rep=NJ)
    for j in range(NJ):
        i = pe.transpose(bank[:, 3, j * P:(j + 1) * P], rt["rep"][:, j].rearrange("p e r -> p (e r)"), ident)
    i.then_inc(ph["cwt_ps"], 1)


def softmax(dve, ph, rt, n):
    def wide(a):
        return a.broadcast_to([P, NJ, n])
    dve.tensor_reduce(rt["m"][:, :, 0:1], rt["lg"][:, :, 0:n], AX.X, ALU.max).then_inc(ph["rmax"], 1)
    need(dve, ph, rmax=1)
    dve.tensor_tensor(rt["sh"][:, :, 0:n], rt["lg"][:, :, 0:n], wide(rt["m"][:, :, 0:1]), ALU.subtract)\
        .then_inc(ph["shifted"], 1)
    need(dve, ph, rexp=1)
    dve.tensor_reduce(rt["m"][:, :, 1:2], rt["ex"][:, :, 0:n], AX.X, ALU.add).then_inc(ph["rsum"], 1)
    need(dve, ph, rsum=1)
    dve.reciprocal(rt["m"][:, :, 2:3], rt["m"][:, :, 1:2]).then_inc(ph["rrec"], 1)
    need(dve, ph, rrec=1)
    dve.tensor_tensor(rt["pr"][:, :, 0:n], rt["ex"][:, :, 0:n], wide(rt["m"][:, :, 2:3]), ALU.mult)\
        .then_inc(ph["prob"], 1)
    need(dve, ph, prob=1)


def top2(dve, ph, rt, src, n, iota):
    for j in range(NJ):
        dve.max(rt["top"][:, j, :], rt[src][:, j, 0:n]).then_inc(ph["top"], 1)
    need(dve, ph, top=NJ)
    for j in range(NJ):
        dve.max_index(rt["idx"][:, j, :], rt["top"][:, j, :], rt[src][:, j, 0:n]).then_inc(ph["idx"], 1)
    need(dve, ph, idx=NJ)
    dve.tensor_copy(rt["idf"][:], rt["idx"][:]).then_inc(ph["idf"], 1)
    need(dve, ph, idf=1)
    io = iota[:, 0:n].unsqueeze(1).broadcast_to([P, NJ, n])
    dve.tensor_tensor(rt["one"][:, :, 0:n], io, rt["idf"][:, :, 0:1].broadcast_to([P, NJ, n]), ALU.is_equal)\
        .then_inc(ph["hot"], 1)
    dve.tensor_tensor(rt["pick"][:, :, 0:n], io, rt["idf"][:, :, 1:2].broadcast_to([P, NJ, n]), ALU.is_equal)\
        .then_inc(ph["hot"], 1)
    need(dve, ph, hot=2)
    dve.tensor_tensor(rt["pick"][:, :, 0:n], rt["pick"][:, :, 0:n], rt["one"][:, :, 0:n], ALU.add)\
        .then_inc(ph["pick"], 1)
    need(dve, ph, pick=1)


def mlp(nc, pool, bank, name, w_dram, x_hi, x_lo, cw, acc):
    pairs = w_dram.shape[0] // 2
    UN = 2 * NS
    with ExitStack() as own:
        def sb(n, shape, dt=F32):
            return own.enter_context(nc.sbuf_tensor(name + n, shape, dt))

        raw = sb("_raw", [P, 2, MLP_W])
        w_hi, w_lo = sb("_whi", [P, 2, MLP_W], F32R), sb("_wlo", [P, 2, MLP_W], F32R)
        sg = sb("_sg", [P, 2, TS])
        su = sb("_su", [P, 2, TS])
        hh = sb("_h", [P, 2, TS]) if cw is not None else su
        h_hi, h_lo = sb("_hhi", [P, 2, TS], F32R), sb("_hlo", [P, 2, TS], F32R)
        ph = Phase(nc, pool)
        SU, LO, H, DOWN, ADDED, SPLIT = 2, 2, 2, 2, 2, 1

        def half(t, j, a):
            return t[:, j, a:a + P]

        def bodies(eng, emit):
            emit(0, True, pairs == 1)
            if pairs > 2:
                with eng.Fori(1, pairs - 1) as i:
                    emit(i, False, False)
            if pairs > 1:
                emit(pairs - 1, False, True)

        with nc.Block(no_gpsimd_drain=True) as block:

            @block.sync
            def _(sp):
                def emit(i, first, last):
                    for j in range(2):
                        sp.wait_ge(ph[f"split{j}"], i + SPLIT)
                        src = w_dram[bass.ds(i * 2 + j, 1)].rearrange("o p c -> (o p) c")
                        sp.dma_start(raw[:, j, :], src).then_inc(ph[f"raw{j}"], 16)
                sp.sem_inc(ph["split0"], SPLIT)
                sp.sem_inc(ph["split1"], SPLIT)
                bodies(sp, emit)
                sp.wait_ge(ph["raw0"], 16 * pairs)
                sp.wait_ge(ph["raw1"], 16 * pairs)

            @block.tensor
            def _(pe):
                def gate_and_up(j, c, n):
                    pe.wait_ge(ph["su"], n - 2 + 1 + SU)
                    for m in range(2):
                        for k in range(KD):
                            a = (2 * k + m) * P
                            i = mm3(pe, bank[:, 2 * (c % 2) + m, :], (half(w_hi, j, a), half(w_lo, j, a)),
                                    (x_hi[:, k, c * TS:(c + 1) * TS], x_lo[:, k, c * TS:(c + 1) * TS]),
                                    k == 0, k == KD - 1)
                    i.then_inc(ph["gu"], 1)

                def emit(i, first, last):
                    for u in range(UN):
                        n = i * UN + u
                        if u + 1 == NS:
                            pe.wait_ge(ph["split1"], i + 1 + SPLIT)
                        if u + 1 < UN:
                            gate_and_up((u + 1) // NS, (u + 1) % NS, n + 1)
                        elif not last:
                            pe.wait_ge(ph["split0"], i + 2 + SPLIT)
                            gate_and_up(0, 0, n + 1)
                        pe.wait_ge(ph["lo"], n + 1 + LO)
                        pe.wait_ge(ph["added"], n - 2 + 1 + ADDED)
                        for m in range(KD):
                            a = 2 * KD * P + m * P
                            q = mm3(pe, bank[:, 4 + 2 * (u % 2) + m, :], (half(w_hi, u // NS, a), half(w_lo, u // NS, a)),
                                    (h_hi[:, u % 2, :], h_lo[:, u % 2, :]))
                        q.then_inc(ph["down"], 1)
                pe.sem_inc(ph["down"], DOWN)
                pe.wait_ge(ph["split0"], 1 + SPLIT)
                gate_and_up(0, 0, 0)
                bodies(pe, emit)

            @block.scalar
            def _(act):
                def split_high(j, k, done):
                    act.wait_ge(ph[f"raw{j}"], k * 16 + 16)
                    act.wait_ge(ph["down"], done + DOWN)
                    act.activation(w_hi[:, j, :], raw[:, j, :], ACT.Copy).then_inc(ph[f"high{j}"], 1)

                def emit(i, first, last):
                    for u in range(UN):
                        n = i * UN + u
                        c = u % 2
                        act.wait_ge(ph["gu"], n + 1)
                        act.wait_ge(ph["su"], n - 2 + 1 + SU)
                        act.activation(sg[:, c, :], bank[:, 2 * c, :], ACT.Silu).then_inc(ph["silu"], 1)
                        if u == 1:
                            split_high(1, i, i * UN)
                        if u == NS + 1 and not last:
                            split_high(0, i + 1, i * UN + NS)
                        if cw is None:
                            act.wait_ge(ph["su"], n + 1 + SU)
                        else:
                            act.wait_ge(ph["h"], n + 1 + H)
                        act.wait_ge(ph["down"], n - 2 + 1 + DOWN)
                        act.activation(h_hi[:, c, :], hh[:, c, :], ACT.Copy).then_inc(ph["hi"], 1)
                split_high(0, 0, 0)
                bodies(act, emit)

            @block.gpsimd
            def _(pl):
                def emit(i, first, last):
                    for u in range(UN):
                        n = i * UN + u
                        c = u % 2
                        pl.wait_ge(ph["su"], n + 1 + SU)
                        pl.wait_ge(ph["lo"], n - 2 + 1 + LO)
                        pl.tensor_tensor(hh[:, c, :], su[:, c, :], cw[:, (u % NS) * TS:(u % NS + 1) * TS], ALU.mult)\
                            .then_inc(ph["h"], 1)
                if cw is not None:
                    pl.sem_inc(ph["h"], H)
                    bodies(pl, emit)

            @block.vector
            def _(dve):
                def split_low(j, k):
                    dve.wait_ge(ph[f"high{j}"], k + 1)
                    dve.tensor_tensor(w_lo[:, j, :], raw[:, j, :], w_hi[:, j, :].bitcast(F32), ALU.subtract)\
                        .then_inc(ph[f"split{j}"], 1)

                def add(c, n):
                    dve.wait_ge(ph["down"], n + 1 + DOWN)
                    dve.wait_ge(ph["added"], n - 1 + ADDED)
                    s = acc[:, :, c * TS:(c + 1) * TS]
                    dve.tensor_tensor(s, bank[:, 4 + 2 * (c % 2):6 + 2 * (c % 2), :], s, ALU.add).then_inc(ph["added"], 1)

                def emit(i, first, last):
                    for u in range(UN):
                        n = i * UN + u
                        c = u % 2
                        dve.wait_ge(ph["silu"], n + 1)
                        if cw is None:
                            dve.wait_ge(ph["lo"], n - 2 + 1 + LO)
                        else:
                            dve.wait_ge(ph["h"], n - 2 + 1 + H)
                        dve.tensor_tensor(su[:, c, :], bank[:, 2 * c + 1, :], sg[:, c, :], ALU.mult).then_inc(ph["su"], 1)
                        if u == 1:
                            split_low(1, i)
                        if u == NS + 1 and not last:
                            split_low(0, i + 1)
                        if not (first and u == 0):
                            add((u + NS - 1) % NS, n - 1)
                        dve.wait_ge(ph["hi"], n + 1)
                        dve.tensor_tensor(h_lo[:, c, :], hh[:, c, :], h_hi[:, c, :].bitcast(F32), ALU.subtract)\
                            .then_inc(ph["lo"], 1)
                dve.sem_inc(ph["su"], SU)
                dve.sem_inc(ph["lo"], LO)
                dve.sem_inc(ph["added"], ADDED)
                split_low(0, 0)
                bodies(dve, emit)
                add(NS - 1, pairs * UN - 1)
        ph.clear()


def ssm_prepare(nc, pool, bank, wbc, a_dram, acc, e_hi, e_lo, f_hi, f_lo, cw, st, col, colk):
    with ExitStack() as own:
        def sb(name, shape, dt=F32):
            return own.enter_context(nc.sbuf_tensor(name, shape, dt))

        w_raw = sb("bc_raw", [P, KD, D])
        w_hi, w_lo = sb("bc_hi", [P, KD, D], F32R), sb("bc_lo", [P, KD, D], F32R)
        neg_a = sb("neg_a", [HM, 2])
        ph = Phase(nc, pool)
        with nc.Block(no_gpsimd_drain=True) as block:
            @block.sync
            def _(sp):
                sp.dma_start(w_raw[:], wbc).then_inc(ph["raw"], 16)
                sp.wait_ge(ph["raw"], 16)

            @block.scalar
            def _(act):
                act.activation(neg_a[:, 0:1], col("A_log")[0:HM], ACT.Exp).then_inc(ph["exp"], 1)

            @block.vector
            def _(dve):
                need(dve, ph, exp=1)
                dve.tensor_scalar_mul(neg_a[:, 1:2], neg_a[:, 0:1], -1.0)
                need(dve, ph, raw=16)
                dve.tensor_copy(w_hi[:], w_raw[:]).then_inc(ph["hi"], 1)
                need(dve, ph, hi=1)
                dve.tensor_tensor(w_lo[:], w_raw[:], w_hi[:].bitcast(F32), ALU.subtract)
        ph.clear()

        xc, sq = sb("pxc", [P, KD, TS]), sb("psq", [P, KD, TS])
        r = sb("pr", [P, 6, TS])
        xn, hm = sb("pxn", [P, KD, TS]), sb("phm", [P, KD, TS])
        rt = router_tiles(sb, "rt1_")
        b_feat = sb("b_feat", [P, TS])
        q = sb("dt_q", [HM, 12, TS])

        def both(a):
            return a.unsqueeze(1).broadcast_to([P, KD, TS])

        with nc.Fori(0, NS) as s:
            ph = Phase(nc, pool)
            ts = bass.ds(s * TS, TS)
            js4 = bass.ds(s * NJ, NJ)
            absz, ez, u, lnu, d, c, ru, mx, dt, adt, a, rest = (q[:, i, :] for i in range(12))
            with nc.Block(no_gpsimd_drain=True) as block:

                @block.sync
                def _(sp):
                    need(sp, ph, a=1)
                    sp.dma_start(a_dram[:, ts], a).then_inc(ph["a_out"], 16)
                    need(sp, ph, a_out=16)

                @block.tensor
                def _(pe):
                    for k in range(KD):
                        i = pe.matmul(bank[:, 0, :], col("mean"), acc[:, k, ts], start=k == 0, stop=k == KD - 1)
                    i.then_inc(ph["mean"], 1)
                    need(pe, ph, sq=1)
                    for k in range(KD):
                        i = pe.matmul(bank[:, 1, :], col("mean"), sq[:, k, :], start=k == 0, stop=k == KD - 1)
                    i.then_inc(ph["var"], 1)
                    need(pe, ph, xn=1)
                    router_logits(pe, ph, bank, xn, colk("router1"), NE)
                    need(pe, ph, hm=KD)
                    for k in range(KD):
                        i = pe.matmul(bank[0:HM, 6, :], colk("wdt")[:, k, :], hm[:, k, :], start=k == 0, stop=k == KD - 1)
                    i.then_inc(ph["dt_ps"], 1)
                    need(pe, ph, f_hi=1, f_lo=1)
                    for m in range(2):
                        for k in range(KD):
                            cs = slice(m * P, m * P + P)
                            i = mm3(pe, bank[:, 4 + m, :], (w_hi[:, k, cs], w_lo[:, k, cs]),
                                    (f_hi[:, k, ts], f_lo[:, k, ts]), k == 0, k == KD - 1)
                    i.then_inc(ph["bc_ps"], 1)
                    need(pe, ph, b_feat=1)
                    for j in range(NJ):
                        i = pe.transpose(bank[:, 7, j * P:(j + 1) * P], b_feat[:, j * P:(j + 1) * P], col("ident"))
                    i.then_inc(ph["bt_ps"], 1)
                    need(pe, ph, c_feat=1)
                    for j in range(NJ):
                        i = pe.matmul(bank[:, 4, j * P:(j + 1) * P], b_feat[:, j * P:(j + 1) * P],
                                      st["c_feat"][:, bass.ds(s * TS + j * P, P)], start=True, stop=True)
                    i.then_inc(ph["cb_ps"], 1)
                    router_transpose(pe, ph, bank, rt, col("ident"))
                    need(pe, ph, a=1, wend=1)
                    for m, src in ((0, a), (1, rest)):
                        for j in range(NJ):
                            o = (m * NJ + j) * HM
                            i = pe.transpose(bank[:, 6, o:o + HM], src[:, j * P:(j + 1) * P], col("ident")[0:HM, 0:HM])
                    i.then_inc(ph["at_ps"], 1)

                @block.scalar
                def _(act):
                    need(act, ph, xc=1)
                    act.activation(sq[:], xc[:], ACT.Square).then_inc(ph["sq"], 1)
                    need(act, ph, var=1)
                    rsqrt(act, ph, r[:, 5, :], bank[:, 1, :], col("eps5"), "rstd")
                    need(act, ph, vrr=1)
                    rsqrt(act, ph, r[:, 2, :], r[:, 3, :], col("eps5"), "r1")
                    need(act, ph, xn=1)
                    act.activation(e_hi[:, :, ts], xn[:], ACT.Copy).then_inc(ph["xn_hi"], 1)
                    need(act, ph, hm=KD)
                    act.activation(f_hi[:, :, ts], hm[:], ACT.Copy).then_inc(ph["f_hi"], 1)
                    need(act, ph, shifted=1)
                    act.activation(rt["ex"][:], rt["sh"][:], ACT.Exp).then_inc(ph["rexp"], 1)
                    need(act, ph, dt_ps=1)
                    act.activation(absz, bank[0:HM, 6, :], ACT.Abs, bias=col("dt_bias")[0:HM]).then_inc(ph["absz"], 1)
                    need(act, ph, absz=1)
                    act.activation(ez, absz, ACT.Exp, scale=-1.0).then_inc(ph["ez"], 1)
                    need(act, ph, u=1)
                    act.activation(lnu, u, ACT.Ln).then_inc(ph["lnu"], 1)
                    need(act, ph, lnu=1)
                    act.activation(ru, lnu, ACT.Exp, scale=-1.0).then_inc(ph["ru"], 1)
                    need(act, ph, bc_ps=1)
                    act.activation(b_feat[:], bank[:, 4, :], ACT.Copy).then_inc(ph["b_feat"], 1)
                    act.activation(st["c_feat"][:, ts], bank[:, 5, :], ACT.Copy).then_inc(ph["c_feat"], 1)
                    need(act, ph, bt_ps=1)
                    act.activation(st["b_tok"][:, js4, :].rearrange("p j n -> p (j n)"), bank[:, 7, :], ACT.Copy)
                    need(act, ph, rest=1)
                    act.activation(rest, rest, ACT.Exp).then_inc(ph["wend"], 1)
                    need(act, ph, cwt_ps=1)
                    act.activation(cw[:, ts], bank[:, 3, :], ACT.Copy)
                    need(act, ph, at_ps=1)
                    for m, n in ((0, "a_tok"), (1, "w_tok")):
                        act.activation(st[n][:, js4, :].rearrange("p j h -> p (j h)"),
                                       bank[:, 6, m * NJ * HM:(m + 1) * NJ * HM], ACT.Copy)

                @block.gpsimd
                def _(pl):
                    need(pl, ph, xn=1)
                    pl.tensor_tensor(acc[:, :, ts], acc[:, :, ts], xn[:], ALU.add).then_inc(ph["acc"], 1)
                    need(pl, ph, acc=1)

                @block.vector
                def _(dve):
                    need(dve, ph, mean=1)
                    dve.tensor_tensor(xc[:], acc[:, :, ts], both(bank[:, 0, :]), ALU.subtract).then_inc(ph["xc"], 1)
                    need(dve, ph, rstd=1)
                    dve.tensor_tensor(xn[:], xc[:], both(r[:, 5, :]), ALU.mult).then_inc(ph["xn"], 1)
                    dve.tensor_tensor(r[:, 2, :], bank[:, 1, :], r[:, 5, :], ALU.mult).then_inc(ph["vr"], 1)
                    need(dve, ph, vr=1)
                    dve.tensor_tensor(r[:, 3, :], r[:, 2, :], r[:, 5, :], ALU.mult).then_inc(ph["vrr"], 1)
                    need(dve, ph, r1=1, xn=1)
                    for k in range(KD):
                        dve.scalar_tensor_tensor(hm[:, k, :], xn[:, k, :], col("norm_m")[:, k:k + 1], r[:, 2, :],
                                                 ALU.mult, ALU.mult).then_inc(ph["hm"], 1)
                    need(dve, ph, xn_hi=1)
                    dve.tensor_tensor(e_lo[:, :, ts], xn[:], e_hi[:, :, ts].bitcast(F32), ALU.subtract)
                    need(dve, ph, f_hi=1)
                    dve.tensor_tensor(f_lo[:, :, ts], hm[:], f_hi[:, :, ts].bitcast(F32), ALU.subtract).then_inc(ph["f_lo"], 1)
                    need(dve, ph, logits=1)
                    dve.tensor_copy(rt["lg"][:], bank[:, 2, 0:NJ * NE].rearrange("p (j e) -> p j e", j=NJ)).then_inc(ph["lg"], 1)
                    need(dve, ph, lg=1)
                    softmax(dve, ph, rt, NE)
                    top2(dve, ph, rt, "pr", NE, col("iota"))
                    dve.tensor_tensor(rt["m"][:, :, 3:4], rt["top"][:, :, 0:1], rt["top"][:, :, 1:2], ALU.add)\
                        .then_inc(ph["topsum"], 1)
                    need(dve, ph, topsum=1)
                    dve.reciprocal(rt["m"][:, :, 0:1], rt["m"][:, :, 3:4]).then_inc(ph["toprec"], 1)
                    need(dve, ph, toprec=1)
                    dve.tensor_tensor(rt["sh"][:], rt["pr"][:], rt["m"][:, :, 0:1].broadcast_to([P, NJ, NE]), ALU.mult)\
                        .then_inc(ph["scaled"], 1)
                    need(dve, ph, scaled=1)
                    dve.tensor_tensor(rt["ex"][:], rt["sh"][:], rt["pick"][:], ALU.mult).then_inc(ph["comb"], 1)
                    need(dve, ph, comb=1)
                    for j in range(NJ):
                        dve.tensor_copy(rt["rep"][:, j], rt["ex"][:, j].unsqueeze(2).broadcast_to([P, NE, 8]))\
                            .then_inc(ph["rep"], 1)
                    need(dve, ph, ez=1)
                    dve.tensor_scalar_add(u, ez, 1.0).then_inc(ph["u"], 1)
                    dve.tensor_scalar(mx, bank[0:HM, 6, :], col("dt_bias")[0:HM], 0.0, ALU.add, ALU.max).then_inc(ph["mx"], 1)
                    need(dve, ph, u=1)
                    dve.tensor_scalar_add(d, u, -1.0).then_inc(ph["d"], 1)
                    need(dve, ph, d=1, ru=1)
                    dve.tensor_tensor(c, ez, d, ALU.subtract).then_inc(ph["c"], 1)
                    need(dve, ph, c=1)
                    dve.tensor_tensor(d, c, ru, ALU.mult).then_inc(ph["cr"], 1)
                    need(dve, ph, cr=1, lnu=1)
                    dve.tensor_tensor(dt, lnu, d, ALU.add).then_inc(ph["sp"], 1)
                    need(dve, ph, sp=1, mx=1)
                    dve.tensor_tensor(dt, dt, mx, ALU.add).then_inc(ph["dt"], 1)
                    need(dve, ph, dt=1)
                    dve.tensor_scalar_mul(adt, dt, neg_a[:, 1:2]).then_inc(ph["adt"], 1)
                    need(dve, ph, adt=1)
                    dve.tensor_tensor_scan(a, col("scan128")[0:HM], adt, 0.0, ALU.mult, ALU.add).then_inc(ph["a"], 1)
                    need(dve, ph, a=1)
                    a3 = a.rearrange("p (j t) -> p j t", j=NJ)
                    dve.tensor_tensor(rest.rearrange("p (j t) -> p j t", j=NJ),
                                      a3[:, :, P - 1:P].broadcast_to([HM, NJ, P]), a3, ALU.subtract).then_inc(ph["rest"], 1)
                    need(dve, ph, cb_ps=1)
                    dve.tensor_tensor(st["cb"][:, js4, :], bank[:, 4, :].rearrange("p (j t) -> p j t", j=NJ),
                                      col("causal128").unsqueeze(1).broadcast_to([P, NJ, P]), ALU.mult)
            ph.clear()


def ssm(nc, pool, bank, m_dram, a_dram, acc, f_hi, f_lo, st, col):
    with ExitStack() as own:
        def sb(name, shape, dt=F32):
            return own.enter_context(nc.sbuf_tensor(name, shape, dt))

        b_tok, c_feat, cb, a_tok, w_tok = (st[n] for n in ("b_tok", "c_feat", "cb", "a_tok", "w_tok"))
        proj = sb("proj", [P, KD, T])
        y2 = sb("y2", [P, T])
        a_wide = sb("a_wide", [P, 2, T])
        a_feat = sb("a_feat", [P, T])
        raw = sb("m_raw", [P, MP_W])
        wi_hi, wi_lo = sb("wi_hi", [P, MP_IN], F32R), sb("wi_lo", [P, MP_IN], F32R)
        wo = sb("wo", [P, MP_OUT])
        taps = sb("taps", [P, 8])
        prev = sb("prev", [P, 4])
        skip = sb("skip", [P, 1])
        s_init = sb("s_init", [P, P])
        xbuf = sb("xbuf", [P, 2, NR - 1 + TS])
        cv, th = sb("cv", [P, TS]), sb("th", [P, TS])
        xs = sb("xs", [P, 2, TS])
        tz = sb("tz", [P, TS])
        zs = sb("zs", [P, NS, TS])
        x_tok = sb("x_tok", [P, NJ, P])
        xd = sb("xd", [P, NJ, P])
        a_here, w_here = sb("a_here", [P, T // P, 2]), sb("w_here", [P, T // P, 2])
        mt = sb("mt", [P, 2, 2, TS])
        mm = sb("mm", [P, 2, TS])
        dec = sb("dec", [P, 2, 2, NJ])
        state = sb("state_m", [P, 2, NJ, P])
        ea = sb("ea", [P, TS])
        t1, t2, y, ys = sb("t1", [P, TS]), sb("t2", [P, TS]), sb("y", [P, TS]), sb("ys", [P, TS])
        yz = sb("yz", [P, TS])

        ph = Phase(nc, pool)
        CR = {"xb": 1, "c0": 1, "zs": 1, "xs": 1, "xd": 1, "u": 1, "state": NJ + 1, "mm": 1, "ip": 1,
              "intra": 1, "inter": 1, "t1": 1, "t2": 2, "y": 1, "ys": 1, "yz": 3, "y2": 1, "out": 1,
              "added": 1, "skip": 1, "wo": 1, "ea": 1, "x_tok": 1, "arg": 1, "wi_lo": 0}
        OWNER = {"xb": "scalar", "c0": "scalar", "zs": "vector", "xs": "vector", "xd": "gpsimd", "u": "tensor",
                 "state": "vector", "mm": "gpsimd", "ip": "tensor", "intra": "tensor", "inter": "tensor",
                 "t1": "vector", "t2": "vector", "y": "gpsimd", "ys": "scalar", "yz": "gpsimd",
                 "out": "tensor", "skip": "scalar", "wo": "vector", "ea": "scalar", "x_tok": "scalar",
                 "arg": "scalar"}
        N = NCT * NS

        def credit(eng, who):
            for n, o in OWNER.items():
                if o == who:
                    eng.sem_inc(ph[n], CR[n])

        def done(eng, name, g, per=1):
            eng.wait_ge(ph[name], (g + 1) * per + CR.get(name, 0))

        def slots(eng, slot):
            def some(lo, hi):
                return lambda g: lambda k: lo <= g + k < hi
            edge = some(0, N)
            slot(-1, -1, NS - 1, edge(-1))
            for s in range(NS):
                slot(s, 0, s, edge(s))
            with eng.Fori(1, NCT - 1) as t:
                for s in range(NS):
                    slot(t * NS + s, t, s, lambda k: True)
            for s in range(NS):
                slot(N - NS + s, NCT - 1, s, edge(N - NS + s))
            for s in range(3):
                slot(N + s, NCT, s, edge(N + s))

        def step(s):
            return slice(s * TS, (s + 1) * TS)

        with nc.Block(no_gpsimd_drain=True) as block:

            @block.sync
            def _(sp):
                def load_raw(t):
                    sp.dma_start(raw[:], m_dram[bass.ds(t, 1)].rearrange("o p c -> (o p) c")).then_inc(ph["raw"], 16)

                def load_wide(t, s):
                    src = a_dram[bass.ds(t * 2, 2), step(s)]
                    sp.dma_start(a_wide[:, :, step(s)], src.partition_broadcast(P)).then_inc(ph[f"wide{s}"], 16)

                def load_feat(t, s):
                    for h in range(2):
                        src = a_dram[bass.ds(t * 2 + h, 1), step(s)].rearrange("o t -> (o t)")
                        sp.dma_start(a_feat[h * PH:(h + 1) * PH, step(s)], src.partition_broadcast(PH))\
                            .then_inc(ph[f"feat{s}"], 16)

                def next_tile(t):
                    for s in range(NS):
                        g = t * NS + s
                        done(sp, "dec", g)
                        load_wide(t + 1, s)
                        if s == 1:
                            done(sp, "wo", t)
                            done(sp, "skip", t)
                            load_raw(t + 1)
                        if s:
                            done(sp, "ea", g - 1)
                            load_feat(t + 1, s - 1)
                    done(sp, "ea", t * NS + NS - 1)
                    load_feat(t + 1, NS - 1)

                load_raw(0)
                for s in range(NS):
                    load_wide(0, s)
                    load_feat(0, s)
                next_tile(0)
                with sp.Fori(1, NCT - 1) as t:
                    next_tile(t)
                for s in range(NS):
                    sp.wait_ge(ph[f"wide{s}"], 16 * NCT)
                    sp.wait_ge(ph[f"feat{s}"], 32 * NCT)

            @block.tensor
            def _(pe):
                def project_in(g, s):
                    done(pe, "c0", g - 1)
                    done(pe, "zs", g - 1)
                    for m in range(2):
                        for k in range(KD):
                            a = slice((2 * k + m) * P, (2 * k + m) * P + P)
                            i = mm3(pe, bank[:, m, :], (wi_hi[:, a], wi_lo[:, a]),
                                    (f_hi[:, k, step(s)], f_lo[:, k, step(s)]), k == 0, k == KD - 1)
                    i.then_inc(ph["ip"], 1)

                def turn(g, s):
                    done(pe, "xs", g)
                    done(pe, "x_tok", g - 1)
                    for j in range(NJ):
                        i = pe.transpose(bank[:, 2, j * P:(j + 1) * P], xs[:, s % 2, j * P:(j + 1) * P], col("ident"))
                    i.then_inc(ph["xt"], 1)

                def update(g, s):
                    done(pe, "xd", g)
                    done(pe, "state", g - 1, NJ)
                    for j in range(NJ):
                        i = pe.matmul(bank[:, 5, j * P:(j + 1) * P], b_tok[:, s * NJ + j, :], xd[:, j, :],
                                      start=True, stop=True)
                    i.then_inc(ph["u"], 1)

                def scores(g, s):
                    done(pe, "mm", g)
                    done(pe, "x_tok", g)
                    done(pe, "t2", g - 1)
                    for j in range(NJ):
                        for h in range(2):
                            i = pe.matmul(bank[h * PH:(h + 1) * PH, 3, j * P:(j + 1) * P],
                                          x_tok[:, j, h * PH:(h + 1) * PH], mm[:, h, j * P:(j + 1) * P], start=True, stop=True)
                    i.then_inc(ph["intra"], 1)

                def from_state(g, s):
                    done(pe, "state", g, NJ)
                    done(pe, "t1", g - 1)
                    for j in range(NJ):
                        if j:
                            before = state[:, s % 2, j - 1, :]
                        else:
                            before = state[:, 1 - s % 2, NJ - 1, :] if s else s_init[:]
                        a = s * TS + j * P
                        i = pe.matmul(bank[:, 4, j * P:(j + 1) * P], before, c_feat[:, a:a + P], start=True, stop=True)
                    i.then_inc(ph["inter"], 1)

                def project_out(g):
                    done(pe, "yz", g)
                    done(pe, "added", g - 1)
                    for m in range(KD):
                        i = pe.matmul(bank[:, 6 + m, :], wo[:, m * P:(m + 1) * P], yz[:], start=True, stop=True)
                    i.then_inc(ph["out"], 1)

                def slot(g, t, s, has):
                    if has(1):
                        if s == NS - 1:
                            done(pe, "wi_lo", t + 1)
                        project_in(g + 1, (s + 1) % NS)
                    if has(0):
                        turn(g, s)
                    if has(-1):
                        from_state(g - 1, (s - 1) % NS)
                    if has(-2):
                        if s == 2:
                            done(pe, "wo", t)
                        project_out(g - 2)
                    if has(0):
                        update(g, s)
                        scores(g, s)

                credit(pe, "tensor")
                slots(pe, slot)
                done(pe, "y2", N - 1)
                for s in range(NS):
                    i = pe.matmul(bank[:, s, :], col("mean_di"), y2[:, step(s)], start=True, stop=True)
                i.then_inc(ph["yms"], 1)

            @block.scalar
            def _(act):
                def take_weights(t):
                    act.wait_ge(ph["raw"], t * 16 + 16)
                    done(act, "ip", t * NS - 1)
                    act.activation(wi_hi[:], raw[:, 0:MP_IN], ACT.Copy).then_inc(ph["wi_hi"], 1)

                def take_vectors(t, head):
                    if not head:
                        done(act, "inter", t * NS - NS)
                    act.activation(taps[:, 0:5], raw[:, MP_VEC:MP_VEC + 5], ACT.Copy, scale=0.5)
                    act.activation(prev[:, 0:3], raw[:, MP_CS:MP_CS + 3], ACT.Copy)
                    act.activation(s_init[:], raw[:, MP_ST:MP_ST + P], ACT.Copy).then_inc(ph["vec"], 1)

                def differences(g, t, s):
                    if s == 0:
                        done(act, "arg", g - 1)
                        act.activation(a_here[:], a_tok[:, :, bass.ds(t * 2, 2)], ACT.Copy).then_inc(ph["a_here"], 1)
                        done(act, "a_here", t)
                    act.wait_ge(ph[f"wide{s}"], (t + 1) * 16)
                    done(act, "mm", g - 2)
                    for h in range(2):
                        for j in range(NJ):
                            a = s * TS + j * P
                            i = act.activation(mt[:, s % 2, h, j * P:(j + 1) * P], a_wide[:, h, a:a + P], ACT.Relu,
                                               bias=a_here[:, s * NJ + j, h:h + 1], scale=-1.0)
                    i.then_inc(ph["arg"], 1)

                def gate(g):
                    done(act, "ip", g)
                    done(act, "zs", g - 1)
                    act.activation(tz[:], bank[:, 0, :], ACT.Tanh, scale=0.5).then_inc(ph["tz"], 1)

                def tokens(g):
                    done(act, "xt", g)
                    done(act, "intra", g - 1)
                    done(act, "xd", g - 1)
                    act.activation(x_tok[:].rearrange("p j c -> p (j c)"), bank[:, 2, :], ACT.Copy)\
                        .then_inc(ph["x_tok"], 1)

                def convolve(g, t, s):
                    c = s % 2
                    done(act, "ip", g)
                    done(act, "xs", g - 1)
                    done(act, "vec", t)
                    act.wait_ge(ph["xb"], g + CR["xb"])
                    before = xbuf[:, 1 - c, TS:TS + 3] if s else prev[:, 0:3]
                    act.activation(xbuf[:, c, 0:3], before, ACT.Copy)
                    act.activation(xbuf[:, c, 3:3 + TS], bank[:, 1, :], ACT.Copy).then_inc(ph["xb"], 1)
                    act.activation(cv[:], bank[:, 1, :], ACT.Identity, bias=taps[:, 4:5], scale=taps[:, 3:4])\
                        .then_inc(ph["c0"], 1)

                def decays(g, s):
                    done(act, "arg", g)
                    act.activation(mt[:, s % 2], mt[:, s % 2], ACT.Exp, scale=-1.0).then_inc(ph["ex"], 1)
                    done(act, "state", g - 2, NJ)
                    act.activation(dec[:, s % 2], a_wide[:, :, s * TS + P - 1:(s + 1) * TS:P], ACT.Exp).then_inc(ph["dec"], 1)

                def since_start(g, t, s):
                    act.wait_ge(ph[f"feat{s}"], t * 32 + 32)
                    done(act, "t1", g - 1)
                    act.activation(ea[:], a_feat[:, step(s)], ACT.Exp).then_inc(ph["ea"], 1)

                def square(g):
                    done(act, "y", g)
                    done(act, "y2", g - 1)
                    act.activation(ys[:], y[:], ACT.Square).then_inc(ph["ys"], 1)

                def tanh(g):
                    done(act, "tap", g, NR - 1)
                    act.activation(th[:], cv[:], ACT.Tanh).then_inc(ph["th"], 1)

                def slot(g, t, s, has):
                    n, tn = (s + 1) % NS, t + (s == NS - 1)
                    if has(1):
                        differences(g + 1, tn, n)
                        gate(g + 1)
                    if has(0):
                        tokens(g)
                    if has(1):
                        convolve(g + 1, tn, n)
                    if s == NS - 2 and has(2):
                        take_weights(t + 1)
                    if has(1):
                        decays(g + 1, n)
                    if has(0):
                        if s == 0:
                            done(act, "t2", g - 1)
                            act.activation(skip[:], raw[:, MP_VEC + 5:MP_VEC + 6], ACT.Copy).then_inc(ph["skip"], 1)
                        since_start(g, t, s)
                    if has(-1):
                        square(g - 1)
                    if has(1):
                        tanh(g + 1)
                    if s == NS - 2 and has(2):
                        take_vectors(t + 1, False)

                credit(act, "scalar")
                take_weights(0)
                take_vectors(0, True)
                slots(act, slot)
                done(act, "yms", 0)
                rsqrt(act, ph, y2[:], bank[:, 0:NS, :].rearrange("p s t -> p (s t)"), col("eps5"), "yr")

            @block.gpsimd
            def _(pl):
                def decayed(g, s):
                    done(pl, "ex", g)
                    done(pl, "intra", g - 1)
                    pl.tensor_tensor(mm[:], mt[:, s % 2], cb[:, s * NJ:(s + 1) * NJ, :].rearrange("p j t -> p (j t)")
                                     .unsqueeze(1).broadcast_to([P, 2, TS]), ALU.mult).then_inc(ph["mm"], 1)

                def squares(g, s):
                    done(pl, "ys", g)
                    done(pl, "y2", g - 1)
                    pl.tensor_tensor(y2[:, step(s)], y2[:, step(s)], ys[:], ALU.add).then_inc(ph["y2"], 1)

                def to_end(g, t, s):
                    if s == 0:
                        done(pl, "xd", g - 1)
                        pl.tensor_copy(w_here[:], w_tok[:, :, bass.ds(t * 2, 2)]).then_inc(ph["w_here"], 1)
                        done(pl, "w_here", t)
                    done(pl, "x_tok", g)
                    done(pl, "u", g - 1)
                    pl.tensor_tensor(xd[:].rearrange("p j (h c) -> p j h c", h=2),
                                     x_tok[:].rearrange("p j (h c) -> p j h c", h=2),
                                     w_here[:, s * NJ:(s + 1) * NJ, :].unsqueeze(3)
                                     .broadcast_to([P, NJ, 2, PH]), ALU.mult).then_inc(ph["xd"], 1)

                def outputs(g, s):
                    done(pl, "t1", g)
                    done(pl, "t2", g)
                    done(pl, "ys", g - 1)
                    done(pl, "yz", g - 1)
                    pl.tensor_tensor(y[:], t1[:], t2[:], ALU.add).then_inc(ph["y"], 1)
                    done(pl, "y", g)
                    done(pl, "zs", g)
                    done(pl, "out", g - 1)
                    pl.tensor_tensor(yz[:], y[:], zs[:, s], ALU.mult).then_inc(ph["yz"], 1)

                def slot(g, t, s, has):
                    if has(0):
                        decayed(g, s)
                    if has(-2):
                        squares(g - 2, (s - 2) % NS)
                    if has(0):
                        to_end(g, t, s)
                    if has(-1):
                        outputs(g - 1, (s - 1) % NS)

                pl.memset(y2[:], 0.0).then_inc(ph["y2"], 1)
                credit(pl, "gpsimd")
                slots(pl, slot)
                done(pl, "y2", N - 1)

            @block.vector
            def _(dve):
                def low_in(t):
                    done(dve, "wi_hi", t)
                    dve.tensor_tensor(wi_lo[:], raw[:, 0:MP_IN], wi_hi[:].bitcast(F32), ALU.subtract).then_inc(ph["wi_lo"], 1)

                def gate(g, s):
                    done(dve, "tz", g)
                    done(dve, "yz", g - NS)
                    dve.scalar_tensor_tensor(zs[:, s], tz[:], 1.0, bank[:, 0, :], ALU.add, ALU.mult).then_inc(ph["zs"], 1)

                def convolve(g, s):
                    done(dve, "xb", g)
                    done(dve, "c0", g)
                    for k in range(NR - 1):
                        if k:
                            dve.wait_ge(ph["tap"], g * (NR - 1) + k)
                        dve.scalar_tensor_tensor(cv[:], xbuf[:, s % 2, k:k + TS], taps[:, k:k + 1], cv[:], ALU.mult, ALU.add)\
                            .then_inc(ph["tap"], 1)

                def silu(g, s):
                    done(dve, "th", g)
                    done(dve, "t2", g - 2)
                    dve.scalar_tensor_tensor(xs[:, s % 2], th[:], 1.0, cv[:], ALU.add, ALU.mult).then_inc(ph["xs"], 1)

                def add(g, s):
                    done(dve, "out", g)
                    done(dve, "added", g - 1)
                    dve.tensor_tensor(proj[:, :, step(s)], bank[:, 6:8, :], proj[:, :, step(s)], ALU.add)\
                        .then_inc(ph["added"], 1)

                def scan(g, t, s):
                    done(dve, "u", g)
                    done(dve, "dec", g)
                    done(dve, "inter", g - 1)
                    if s == 0:
                        done(dve, "vec", t)
                    for j in range(NJ):
                        dve.wait_ge(ph["state"], g * NJ + j + CR["state"])
                        if j:
                            before = state[:, s % 2, j - 1]
                        else:
                            before = state[:, 1 - s % 2, NJ - 1] if s else s_init[:]
                        for h in range(2):
                            hs = slice(h * PH, (h + 1) * PH)
                            i = dve.scalar_tensor_tensor(state[:, s % 2, j, hs], before[:, hs], dec[:, s % 2, h, j:j + 1],
                                                         bank[:, 5, j * P + h * PH:j * P + (h + 1) * PH], ALU.mult, ALU.add)
                        i.then_inc(ph["state"], 1)

                def own_tokens(g, s):
                    done(dve, "intra", g)
                    done(dve, "y", g - 1)
                    dve.scalar_tensor_tensor(t2[:], xs[:, s % 2], skip[:], bank[:, 3, :], ALU.mult, ALU.add)\
                        .then_inc(ph["t2"], 1)

                def state_part(g):
                    done(dve, "inter", g)
                    done(dve, "ea", g)
                    done(dve, "y", g - 1)
                    dve.tensor_tensor(t1[:], bank[:, 4, :], ea[:], ALU.mult).then_inc(ph["t1"], 1)

                def slot(g, t, s, has):
                    if has(-3):
                        add(g - 3, (s - 3) % NS)
                    if has(-1):
                        done(dve, "skip", t - (s == 0))
                        own_tokens(g - 1, (s - 1) % NS)
                    if has(1):
                        gate(g + 1, (s + 1) % NS)
                    if has(-1):
                        state_part(g - 1)
                    if has(1):
                        convolve(g + 1, (s + 1) % NS)
                    if s == NS - 2 and has(2):
                        low_in(t + 1)
                    if s == 1 and has(0):
                        dve.wait_ge(ph["raw"], t * 16 + 16)
                        done(dve, "out", g - 2)
                        dve.tensor_scalar(wo[:], raw[:, MP_IN:MP_VEC], raw[:, MP_VEC + 6:MP_VEC + 7], 0.5,
                                          ALU.mult, ALU.mult).then_inc(ph["wo"], 1)
                    if has(0):
                        scan(g, t, s)
                    if has(1):
                        silu(g + 1, (s + 1) % NS)

                dve.memset(proj[:], 0.0).then_inc(ph["added"], 1)
                credit(dve, "vector")
                low_in(0)
                slots(dve, slot)
                done(dve, "yr", 0)
                done(dve, "added", N - 1)
                dve.tensor_tensor(proj[:], proj[:], y2[:].unsqueeze(1).broadcast_to([P, KD, T]), ALU.mult)\
                    .then_inc(ph["yr"], 1)
                done(dve, "yr", 1)
                dve.tensor_tensor(acc[:], acc[:], proj[:], ALU.add)
        ph.clear()


def kernel(**inputs):
    import numpy as np
    import concourse.bacc as bacc
    from concourse.bass_utils import run_bass_kernel_spmd as run

    w = {n: np.asarray(a) for n, a in inputs.items()}

    def feat(a):
        return a.reshape(KD, P, -1).transpose(1, 0, 2)

    x = w["L0_attn_x"]
    arrays = {"xT": x.transpose(0, 2, 1).reshape(B, KD, P, T).transpose(0, 2, 1, 3)}

    tab = np.zeros((P, TABLE_W), np.float32)

    def put(name, a):
        a = np.asarray(a, np.float32)
        a0, _ = _cols[name]
        a = a.reshape(a.shape[0], -1)
        tab[0:a.shape[0], a0:a0 + a.shape[1]] = a

    p, f = np.arange(P)[:, None], np.arange(TS)[None, :]
    put("ident", np.eye(P))
    put("mean", np.full((P, P), 1.0 / D))
    put("mean32", (p // HV == f[:, :P] // HV) / float(HV))
    put("mean_di", np.full((P, P), 1.0 / DI))
    put("scan64", np.broadcast_to(f % CH != 0, (P, TS)))
    put("scan128", np.broadcast_to(f % P != 0, (P, TS)))
    put("causal64", p % CH <= f[:, :CH])
    put("causal128", p <= f[:, :P])
    put("headmask", p // HK == f[:, :H0])
    put("bdmask", p // HK == f[:, :D] // HV)
    put("iota", np.broadcast_to(f[:, :NE], (P, NE)))
    put("bias0", np.broadcast_to(w["L0_ffn_extra_bias"], (P, E0)))
    put("scale0", np.broadcast_to(w["L0_ffn_extra_scale"], (P, E0)))
    put("norm1", feat(w["L0_attn_norm1_w"]))
    put("ffn_norm", feat(w["L0_attn_ffn_norm_w"]))
    put("norm_m", feat(w["L1_attn_norm_w"]))
    put("eps6", np.full((P, 1), 1e-6))
    put("eps5", np.full((P, 1), 1e-5))
    put("gk_b", w["L0_attn_gk_b"][:, None])
    put("gnorm", np.tile(w["L0_attn_gnorm_w"], P // HV)[:, None])
    put("dt_bias", w["L1_attn_dt_bias"][:, None])
    put("A_log", w["L1_attn_A_log"][:, None])
    put("router0", feat(np.concatenate([w["L0_ffn_cls_w"].T, w["L0_ffn_gate_w"].T], 1)))
    put("router1", feat(w["L1_ffn_router_w"]))
    put("gk1", feat(w["L0_attn_gk_w1"]))
    put("gk2", w["L0_attn_gk_w2"])
    win = w["L1_attn_in_proj_w"]
    put("wdt", feat(win[2 * DI + 2 * NST:].T))
    arrays["table"] = tab

    arrays["gla_w"] = feat(np.concatenate([w["L0_attn_wq"], w["L0_attn_wk"], w["L0_attn_wg"], w["L0_attn_wv"]], 1))
    arrays["gla_wo"] = feat(w["L0_attn_wo"])
    arrays["wbc"] = feat(win[2 * DI:2 * DI + 2 * NST].T)

    def hidden_tiles(gate, up, down):
        n = gate.shape[0] // P
        gu = np.stack([gate, up]).reshape(2, n, P, KD, P).transpose(1, 4, 3, 0, 2).reshape(n, P, -1)
        return np.concatenate([gu, down.reshape(n, P, D)], 2)

    def by_expert(a):
        return a.reshape(NE, -1, 8, D).transpose(1, 0, 2, 3).reshape(-1, D)

    def padded(a):
        n = -a.shape[0] % (2 * P)
        return np.concatenate([a, np.zeros((n, D), a.dtype)])

    arrays["ffn0"] = hidden_tiles(padded(w["L0_attn_w_gate"].T), padded(w["L0_attn_w_up"].T), padded(w["L0_attn_w_down"]))
    parts = []
    for routed, shared, down in (("wg", "sg", False), ("wu", "su", False), ("wd", "sd", True)):
        r, s = w["L0_ffn_" + routed], w["L0_ffn_" + shared]
        if down:
            r, s = r.transpose(0, 2, 1), s.T
        parts.append(by_expert(np.concatenate([r, s.reshape(NE - E0, -1, D)])))
    arrays["moe0"] = hidden_tiles(*parts)
    arrays["moe1"] = hidden_tiles(by_expert(w["L1_ffn_gate_w"].transpose(0, 2, 1)),
                                  by_expert(w["L1_ffn_up_w"].transpose(0, 2, 1)), by_expert(w["L1_ffn_down_w"]))

    zx = win[:2 * DI].reshape(2, NCT, P, KD, P).transpose(1, 4, 3, 0, 2).reshape(NCT, P, -1)
    vec = np.zeros((NCT, P, 8), np.float32)
    vec[:, :, 0:4] = w["L1_attn_conv_w"].reshape(NCT, P, NR)
    vec[:, :, 4] = w["L1_attn_conv_b"].reshape(NCT, P)
    vec[:, :, 5] = np.repeat(w["L1_attn_D_param"], PH).reshape(NCT, P)
    vec[:, :, 6] = w["L1_attn_inner_norm_w"].reshape(NCT, P)
    cs = np.zeros((NCT, P, 4), np.float32)
    cs[:, :, 0:3] = w["L1_attn_conv_state"].reshape(NCT, P, NR - 1)
    init = w["L1_attn_ssm_state"].reshape(NCT, 2, NST, PH).transpose(0, 2, 1, 3).reshape(NCT, P, P)
    arrays["mamba"] = np.concatenate([zx, w["L1_attn_out_proj_w"].T.reshape(NCT, P, D), vec, cs, init], 2)

    nc = bacc.Bacc("TRN2", target_bir_lowering=False, num_devices=1)
    arrays = {n: np.ascontiguousarray(a) for n, a in arrays.items()}
    aps = {n: nc.dram_tensor(n + "_dram", a.shape, F32, kind="ExternalInput").ap() for n, a in arrays.items()}
    a_dram = nc.dram_tensor("a_scratch", (HM, T), F32, kind="Internal").ap()
    out = nc.dram_tensor("out_dram", (B, P, KD, T), F32, kind="ExternalOutput").ap()
    program(nc, a_dram=a_dram, outT=out, **aps)
    r = run(nc, [{n + "_dram": a for n, a in arrays.items()}], core_ids=[0])
    y = r.results[0]["out_dram"]
    return np.ascontiguousarray(y.transpose(0, 2, 1, 3).reshape(B, D, T).transpose(0, 2, 1))
```
